# Optimizing a Trainium2 kernel written in Bass

```python
import numpy as np
import jax
import jax.numpy as jnp

def _softmax(x, axis=-1):
    return jax.nn.softmax(x, axis=axis)

def _gelu(x):
    return jax.nn.gelu(x, approximate=True)

def _silu(x):
    return jax.nn.silu(x)

def _sigmoid(x):
    return jax.nn.sigmoid(x)

def _layernorm(x, axis=-1, eps=1e-05):
    m = jnp.mean(x, axis=axis, keepdims=True)
    v = jnp.var(x, axis=axis, keepdims=True)
    return (x - m) / jnp.sqrt(v + eps)

def _scatter_add(tgt, idx, src, axis=0):
    return tgt.at[idx].add(src)

def _segment_sum(src, seg, n):
    return jax.ops.segment_sum(src, seg, n)
kernel_name = 'mk_decoder_postln_d2_seqx_r8_b4ccbd'

def setup_inputs(seed: int=0):
    np.random.seed(seed)
    _w = jnp.asarray

    def _rec_inputs():
        import jax
        import jax.numpy as jnp
        _rk = jax.random.key(seed)
        x = -0.0003929 + 0.9999 * jax.random.normal(jax.random.fold_in(_rk, 1), (16, 128, 128), jnp.float32)
        _lenS = 128 - jax.random.randint(jax.random.fold_in(_rk, 7), (16,), 0, max(1, 128 // 4) + 1, jnp.int32)
        _lenS2 = 128 - jax.random.randint(jax.random.fold_in(_rk, 8), (16,), 0, max(1, 128 // 4) + 1, jnp.int32)
        _ctx_1024P = jax.random.normal(jax.random.fold_in(_rk, 11), (16, 16, 128), jnp.float32)
        _ctx_1024c = jax.random.dirichlet(jax.random.fold_in(_rk, 511), 0.3 * jnp.ones((16,), jnp.float32), (16, 128))
        _ctx_1024t = jnp.einsum('bsk,bkd->bsd', _ctx_1024c, _ctx_1024P)
        _ctx_1024t = _ctx_1024t * jax.lax.rsqrt(jnp.mean(jnp.square(_ctx_1024t)) + 1e-12) * 0.953939
        ctx_1024 = 2.81802e-05 + 1.00001 * (_ctx_1024t + 0.3 * jax.random.normal(jax.random.fold_in(_rk, 611), (16, 128, 128), jnp.float32))
        _validS = jnp.arange(128)[None, :] < _lenS[:, None]
        _validS2 = jnp.arange(128)[None, :] < _lenS2[:, None]
        _causal = jnp.tril(jnp.ones((128, 128), dtype=bool))
        mask_Bx1xSxS2_ff0 = jnp.where(jnp.ones((16, 1, 128, 128), dtype=bool), 0.0, -1000000000.0).astype(jnp.float32)
        return (x, ctx_1024, mask_Bx1xSxS2_ff0)
    x, ctx_1024, mask_Bx1xSxS2_ff0 = _rec_inputs()

    def _L0_attn_setup():
        import jax, jax.numpy as jnp
        import numpy as np
        D_MODEL = 128
        N_HEADS = 16
        D_K = D_MODEL // N_HEADS
        MAX_POS = 64
        ATT_SPAN = MAX_POS
        B, T = (4, 128)
        SCALE_FACTOR = 3

        def _heads(y):
            b, t, _ = y.shape
            return y.reshape(b, t, N_HEADS, D_K).transpose(0, 2, 1, 3)
        key = jax.random.key(seed)
        ks = jax.random.split(key, 16)
        init = lambda k, shape: jax.random.normal(k, shape, dtype=jnp.float32) * 0.02
        inp = {'x': jax.random.normal(ks[0], (B, T, D_MODEL), dtype=jnp.float32), 'Wq': init(ks[1], (D_MODEL, D_MODEL)), 'bq': jnp.zeros((D_MODEL,), jnp.float32), 'Wk': init(ks[2], (D_MODEL, D_MODEL)), 'bk': jnp.zeros((D_MODEL,), jnp.float32), 'Wv': init(ks[3], (D_MODEL, D_MODEL)), 'bv': jnp.zeros((D_MODEL,), jnp.float32), 'Wo': init(ks[4], (D_MODEL, D_MODEL)), 'bo': jnp.zeros((D_MODEL,), jnp.float32), 'Wpk': init(ks[5], (D_MODEL, D_MODEL)), 'bpk': jnp.zeros((D_MODEL,), jnp.float32), 'Wpq': init(ks[6], (D_MODEL, D_MODEL)), 'bpq': jnp.zeros((D_MODEL,), jnp.float32), 'rel_emb': init(ks[7], (2 * ATT_SPAN, D_MODEL))}
        return inp
    _L0_attn_all = _L0_attn_setup()
    _L0_attn_in = {k: v for k, v in _L0_attn_all.items() if k in ('Wq', 'bq', 'Wk', 'bk', 'Wv', 'bv', 'Wo', 'bo', 'Wpk', 'bpk', 'Wpq', 'bpq', 'rel_emb')}
    del _L0_attn_all

    def _L0_xattn_setup():
        import jax, jax.numpy as jnp
        import numpy as np
        GAMMA = 0.96875

        def _decay_matrix(S):
            idx = jnp.arange(S, dtype=jnp.float32)
            dec = GAMMA ** (idx[:, None] - idx[None, :])
            return jnp.triu(dec).T
        key = jax.random.key(seed)
        kq, kk, kv = jax.random.split(key, 3)
        B, S, D = (8, 256, 128)
        Q = jax.random.normal(kq, (B, S, D), dtype=jnp.float32)
        K = jax.random.normal(kk, (B, S, D), dtype=jnp.float32)
        V = jax.random.normal(kv, (B, S, D), dtype=jnp.float32)
        return {'Q': Q, 'K': K, 'V': V}
    _L0_xattn_all = _L0_xattn_setup()
    _L0_xattn_in = {k: v for k, v in _L0_xattn_all.items() if k in ()}
    del _L0_xattn_all

    def _L0_ffn_setup():
        import jax, jax.numpy as jnp
        import numpy as np
        BLOCK = 16
        _GRID = jnp.array([0.0, 0.5, 1.0, 1.5, 2.0, 3.0, 4.0, 6.0], dtype=jnp.float32)
        _MID = jnp.array([0.25, 0.75, 1.25, 1.75, 2.5, 3.5, 5.0], dtype=jnp.float32)

        def fp4_quant_dequant(x):
            shape = x.shape
            xb = x.reshape(shape[:-1] + (shape[-1] // BLOCK, BLOCK))
            scale = jnp.max(jnp.abs(xb), axis=-1, keepdims=True) / 6.0
            scale = jnp.maximum(scale, jnp.float32(1e-12))
            xn = xb / scale
            idx = jnp.searchsorted(_MID, jnp.abs(xn))
            q = _GRID[idx] * jnp.sign(xn) * scale
            return q.reshape(shape)

        def fp4_linear(x, w):
            xq = fp4_quant_dequant(x)
            wq = fp4_quant_dequant(w)
            return jnp.einsum('bsk,nk->bsn', xq, wq)
        key = jax.random.key(seed)
        k1, k2, k3, k4 = jax.random.split(key, 4)
        H, I = (128, 352)
        x = jax.random.normal(k1, (4, 512, H), dtype=jnp.float32)
        w_gate = jax.random.normal(k2, (I, H), dtype=jnp.float32) * 0.02
        w_up = jax.random.normal(k3, (I, H), dtype=jnp.float32) * 0.02
        w_down = jax.random.normal(k4, (H, I), dtype=jnp.float32) * 0.02
        return {'x': x, 'w_gate': w_gate, 'w_up': w_up, 'w_down': w_down}
    _L0_ffn_all = _L0_ffn_setup()
    _L0_ffn_in = {k: v for k, v in _L0_ffn_all.items() if k in ('w_gate', 'w_up', 'w_down')}
    del _L0_ffn_all

    def _L1_attn_setup():
        import jax, jax.numpy as jnp
        import numpy as np
        DIM = 128
        DIM_HEADS = 64
        key = jax.random.key(seed)
        k1, k2, k3 = jax.random.split(key, 3)
        x = jax.random.normal(k1, (1, 256, DIM), dtype=jnp.float32)
        w_qkv = jax.random.normal(k2, (DIM_HEADS * 3, DIM), dtype=jnp.float32) * 0.02
        w_out = jax.random.normal(k3, (DIM, DIM_HEADS), dtype=jnp.float32) * 0.02
        return {'x': x, 'w_qkv': w_qkv, 'w_out': w_out}
    _L1_attn_all = _L1_attn_setup()
    _L1_attn_in = {k: v for k, v in _L1_attn_all.items() if k in ('w_qkv', 'w_out')}
    del _L1_attn_all

    def _L1_xattn_setup():
        import jax, jax.numpy as jnp
        import numpy as np
        EMBED = 128
        HEADS = 16
        HEAD_DIM = EMBED // HEADS
        B, S = (2, 256)
        WINDOW = 128

        def _sliding_window_mask(seq_len, window_size):
            i = jnp.arange(seq_len)[:, None]
            j = jnp.arange(seq_len)[None, :]
            half = window_size // 2
            allowed = (j >= i - half) & (j <= i + half)
            return jnp.where(allowed, 0.0, -jnp.inf).astype(jnp.float32)
        key = jax.random.key(seed)
        ks = jax.random.split(key, 8)
        inp = {'values': jax.random.normal(ks[0], (B, S, EMBED), jnp.float32), 'keys': jax.random.normal(ks[1], (B, S, EMBED), jnp.float32), 'query': jax.random.normal(ks[2], (B, S, EMBED), jnp.float32), 'mask': jnp.zeros((B, 1, S, S), jnp.float32), 'Wq': jax.random.normal(ks[3], (HEAD_DIM, HEAD_DIM), jnp.float32) * (1.0 / np.sqrt(HEAD_DIM)), 'Wk': jax.random.normal(ks[4], (HEAD_DIM, HEAD_DIM), jnp.float32) * (1.0 / np.sqrt(HEAD_DIM)), 'Wv': jax.random.normal(ks[5], (HEAD_DIM, HEAD_DIM), jnp.float32) * (1.0 / np.sqrt(HEAD_DIM)), 'Wo': jax.random.normal(ks[6], (EMBED, EMBED), jnp.float32) * (1.0 / np.sqrt(EMBED)), 'bo': jnp.zeros((EMBED,), jnp.float32), 'num_heads': HEADS}
        return inp
    _L1_xattn_all = _L1_xattn_setup()
    _L1_xattn_in = {k: v for k, v in _L1_xattn_all.items() if k in ('Wq', 'Wk', 'Wv', 'Wo', 'bo')}
    del _L1_xattn_all

    def _L1_ffn_setup():
        import jax, jax.numpy as jnp
        import numpy as np
        NHEAD = 16
        NUM_GROUPS = 4
        EXPERTS_PER_GROUP = 2
        LN_EPS = 1e-05

        def _layernorm(x, g, b):
            mu = jnp.mean(x, axis=-1, keepdims=True)
            var = jnp.mean(jnp.square(x - mu), axis=-1, keepdims=True)
            return (x - mu) * jax.lax.rsqrt(var + LN_EPS) * g + b

        def _mha(x, wi, bi, wo, bo):
            B, S, D = x.shape
            hd = D // NHEAD
            qkv = x @ wi.T + bi
            q, k, v = jnp.split(qkv, 3, axis=-1)

            def heads(t):
                return t.reshape(B, S, NHEAD, hd).transpose(0, 2, 1, 3)
            q, k, v = (heads(q), heads(k), heads(v))
            scores = jnp.einsum('bhqd,bhkd->bhqk', q, k) / jnp.sqrt(jnp.asarray(hd, x.dtype))
            attn = jax.nn.softmax(scores, axis=-1)
            o = jnp.einsum('bhqk,bhkd->bhqd', attn, v)
            o = o.transpose(0, 2, 1, 3).reshape(B, S, D)
            return o @ wo.T + bo

        def _hier_moe(x, w_group, b_group, w_expert, b_expert, w1, b1, w2, b2):
            B, S, D = x.shape
            xt = x.reshape(B * S, D)
            T = xt.shape[0]
            E = NUM_GROUPS * EXPERTS_PER_GROUP
            gp = jax.nn.softmax(xt @ w_group + b_group, axis=-1)
            g_idx = jnp.argmax(gp, axis=-1)
            g_prob = jnp.max(gp, axis=-1)
            elog = jnp.einsum('td,gde->tge', xt, w_expert) + b_expert
            ep = jax.nn.softmax(elog, axis=-1)
            ep_sel = jnp.take_along_axis(ep, g_idx[:, None, None], axis=1)[:, 0, :]
            e_idx_local = jnp.argmax(ep_sel, axis=-1)
            e_prob = jnp.max(ep_sel, axis=-1)
            flat_e = g_idx * EXPERTS_PER_GROUP + e_idx_local
            combine = jax.nn.one_hot(flat_e, E, dtype=xt.dtype) * (g_prob * e_prob)[:, None]
            h = jax.nn.relu(jnp.einsum('td,edf->etf', xt, w1) + b1[:, None, :])
            y = jnp.einsum('etf,efd->etd', h, w2) + b2[:, None, :]
            out = jnp.einsum('te,etd->td', combine, y)
            return out.reshape(B, S, D)
        key = jax.random.key(seed)
        ks = jax.random.split(key, 8)
        B, S, D, F = (2, 128, 128, 256)
        G, Epg = (NUM_GROUPS, EXPERTS_PER_GROUP)
        E = G * Epg
        sc = lambda fan: 1.0 / np.sqrt(fan)
        return {'x': jax.random.normal(ks[0], (B, S, D), jnp.float32), 'in_proj_w': jax.random.normal(ks[1], (3 * D, D), jnp.float32) * sc(D), 'in_proj_b': jnp.zeros((3 * D,), jnp.float32), 'out_proj_w': jax.random.normal(ks[2], (D, D), jnp.float32) * sc(D), 'out_proj_b': jnp.zeros((D,), jnp.float32), 'ln1_g': jnp.ones((D,), jnp.float32), 'ln1_b': jnp.zeros((D,), jnp.float32), 'ln2_g': jnp.ones((D,), jnp.float32), 'ln2_b': jnp.zeros((D,), jnp.float32), 'w_group': jax.random.normal(ks[3], (D, G), jnp.float32) * sc(D), 'b_group': jnp.zeros((G,), jnp.float32), 'w_expert': jax.random.normal(ks[4], (G, D, Epg), jnp.float32) * sc(D), 'b_expert': jnp.zeros((G, Epg), jnp.float32), 'w1': jax.random.normal(ks[5], (E, D, F), jnp.float32) * sc(D), 'b1': jnp.zeros((E, F), jnp.float32), 'w2': jax.random.normal(ks[6], (E, F, D), jnp.float32) * sc(F), 'b2': jnp.zeros((E, D), jnp.float32)}
    _L1_ffn_all = _L1_ffn_setup()
    _L1_ffn_in = {k: v for k, v in _L1_ffn_all.items() if k in ('in_proj_w', 'in_proj_b', 'out_proj_w', 'out_proj_b', 'ln1_g', 'ln1_b', 'ln2_g', 'ln2_b', 'w_group', 'b_group', 'w_expert', 'b_expert', 'w1', 'b1', 'w2', 'b2')}
    del _L1_ffn_all
    return {'x': x, 'ctx_1024': ctx_1024, 'mask_Bx1xSxS2_ff0': mask_Bx1xSxS2_ff0, 'L0_attn_Wq': _L0_attn_in['Wq'], 'L0_attn_bq': _L0_attn_in['bq'], 'L0_attn_Wk': _L0_attn_in['Wk'], 'L0_attn_bk': _L0_attn_in['bk'], 'L0_attn_Wv': _L0_attn_in['Wv'], 'L0_attn_bv': _L0_attn_in['bv'], 'L0_attn_Wo': _L0_attn_in['Wo'], 'L0_attn_bo': _L0_attn_in['bo'], 'L0_attn_Wpk': _L0_attn_in['Wpk'], 'L0_attn_bpk': _L0_attn_in['bpk'], 'L0_attn_Wpq': _L0_attn_in['Wpq'], 'L0_attn_bpq': _L0_attn_in['bpq'], 'L0_attn_rel_emb': _L0_attn_in['rel_emb'], 'L0_ffn_w_gate': _L0_ffn_in['w_gate'], 'L0_ffn_w_up': _L0_ffn_in['w_up'], 'L0_ffn_w_down': _L0_ffn_in['w_down'], 'L1_attn_w_qkv': _L1_attn_in['w_qkv'], 'L1_attn_w_out': _L1_attn_in['w_out'], 'L1_xattn_Wq': _L1_xattn_in['Wq'], 'L1_xattn_Wk': _L1_xattn_in['Wk'], 'L1_xattn_Wv': _L1_xattn_in['Wv'], 'L1_xattn_Wo': _L1_xattn_in['Wo'], 'L1_xattn_bo': _L1_xattn_in['bo'], 'L1_ffn_in_proj_w': _L1_ffn_in['in_proj_w'], 'L1_ffn_in_proj_b': _L1_ffn_in['in_proj_b'], 'L1_ffn_out_proj_w': _L1_ffn_in['out_proj_w'], 'L1_ffn_out_proj_b': _L1_ffn_in['out_proj_b'], 'L1_ffn_ln1_g': _L1_ffn_in['ln1_g'], 'L1_ffn_ln1_b': _L1_ffn_in['ln1_b'], 'L1_ffn_ln2_g': _L1_ffn_in['ln2_g'], 'L1_ffn_ln2_b': _L1_ffn_in['ln2_b'], 'L1_ffn_w_group': _L1_ffn_in['w_group'], 'L1_ffn_b_group': _L1_ffn_in['b_group'], 'L1_ffn_w_expert': _L1_ffn_in['w_expert'], 'L1_ffn_b_expert': _L1_ffn_in['b_expert'], 'L1_ffn_w1': _L1_ffn_in['w1'], 'L1_ffn_b1': _L1_ffn_in['b1'], 'L1_ffn_w2': _L1_ffn_in['w2'], 'L1_ffn_b2': _L1_ffn_in['b2']}

def reference(x, ctx_1024, mask_Bx1xSxS2_ff0, L0_attn_Wq, L0_attn_bq, L0_attn_Wk, L0_attn_bk, L0_attn_Wv, L0_attn_bv, L0_attn_Wo, L0_attn_bo, L0_attn_Wpk, L0_attn_bpk, L0_attn_Wpq, L0_attn_bpq, L0_attn_rel_emb, L0_ffn_w_gate, L0_ffn_w_up, L0_ffn_w_down, L1_attn_w_qkv, L1_attn_w_out, L1_xattn_Wq, L1_xattn_Wk, L1_xattn_Wv, L1_xattn_Wo, L1_xattn_bo, L1_ffn_in_proj_w, L1_ffn_in_proj_b, L1_ffn_out_proj_w, L1_ffn_out_proj_b, L1_ffn_ln1_g, L1_ffn_ln1_b, L1_ffn_ln2_g, L1_ffn_ln2_b, L1_ffn_w_group, L1_ffn_b_group, L1_ffn_w_expert, L1_ffn_b_expert, L1_ffn_w1, L1_ffn_b1, L1_ffn_w2, L1_ffn_b2):
    import jax
    import jax.numpy as jnp

    def _L0_attn_ref(x, Wq, bq, Wk, bk, Wv, bv, Wo, bo, Wpk, bpk, Wpq, bpq, rel_emb):
        import jax, jax.numpy as jnp
        import numpy as np
        D_MODEL = 128
        N_HEADS = 16
        D_K = D_MODEL // N_HEADS
        MAX_POS = 64
        ATT_SPAN = MAX_POS
        B, T = (4, 128)
        SCALE_FACTOR = 3

        def _heads(y):
            b, t, _ = y.shape
            return y.reshape(b, t, N_HEADS, D_K).transpose(0, 2, 1, 3)
        b, t, c = x.shape
        scale = 1.0 / jnp.sqrt(jnp.asarray(D_K * SCALE_FACTOR, x.dtype))
        Q = _heads(x @ Wq.T + bq)
        K = _heads(x @ Wk.T + bk)
        V = _heads(x @ Wv.T + bv)
        rel = jnp.arange(t)[None, :] - jnp.arange(t)[:, None]
        rel_pos = jnp.clip(rel + ATT_SPAN, 0, 2 * ATT_SPAN - 1)
        p2c_pos = jnp.clip(-rel + ATT_SPAN, 0, 2 * ATT_SPAN - 1)
        scores = jnp.einsum('bhqd,bhkd->bhqk', Q, K) * scale
        pos_key = (rel_emb @ Wpk.T + bpk).reshape(2 * ATT_SPAN, N_HEADS, D_K)
        c2p = jnp.einsum('bhqd,shd->bhqs', Q, pos_key) * scale
        c2p = jnp.take_along_axis(c2p, rel_pos[None, None, :, :], axis=-1)
        pos_query = (rel_emb @ Wpq.T + bpq).reshape(2 * ATT_SPAN, N_HEADS, D_K)
        p2c = jnp.einsum('bhkd,shd->bhks', K, pos_query) * scale
        p2c = jnp.take_along_axis(p2c, p2c_pos[None, None, :, :], axis=-1)
        p2c = jnp.swapaxes(p2c, -1, -2)
        scores = scores + c2p + p2c
        probs = jax.nn.softmax(scores, axis=-1)
        ctx = jnp.einsum('bhqk,bhkd->bhqd', probs, V)
        ctx = ctx.transpose(0, 2, 1, 3).reshape(b, t, c)
        return ctx @ Wo.T + bo

    def _L0_xattn_ref(Q, K, V):
        import jax, jax.numpy as jnp
        import numpy as np
        GAMMA = 0.96875

        def _decay_matrix(S):
            idx = jnp.arange(S, dtype=jnp.float32)
            dec = GAMMA ** (idx[:, None] - idx[None, :])
            return jnp.triu(dec).T
        B, S, d = Q.shape
        x = jnp.einsum('bsd,btd->bst', Q, K) / d ** 0.5
        Dm = _decay_matrix(S)
        Dm = Dm / jnp.sqrt(jnp.sum(Dm, axis=1))
        x = x * Dm
        v = jnp.maximum(jnp.abs(jnp.sum(x, axis=-1)), 1.0)
        x = x / v[:, None, :]
        return jnp.einsum('bst,btd->bsd', x, V)

    def _L0_ffn_ref(x, w_gate, w_up, w_down):
        import jax, jax.numpy as jnp
        import numpy as np
        BLOCK = 16
        _GRID = jnp.array([0.0, 0.5, 1.0, 1.5, 2.0, 3.0, 4.0, 6.0], dtype=jnp.float32)
        _MID = jnp.array([0.25, 0.75, 1.25, 1.75, 2.5, 3.5, 5.0], dtype=jnp.float32)

        def fp4_quant_dequant(x):
            shape = x.shape
            xb = x.reshape(shape[:-1] + (shape[-1] // BLOCK, BLOCK))
            scale = jnp.max(jnp.abs(xb), axis=-1, keepdims=True) / 6.0
            scale = jnp.maximum(scale, jnp.float32(1e-12))
            xn = xb / scale
            idx = jnp.searchsorted(_MID, jnp.abs(xn))
            q = _GRID[idx] * jnp.sign(xn) * scale
            return q.reshape(shape)

        def fp4_linear(x, w):
            xq = fp4_quant_dequant(x)
            wq = fp4_quant_dequant(w)
            return jnp.einsum('bsk,nk->bsn', xq, wq)
        gate = fp4_linear(x, w_gate)
        y = fp4_linear(x, w_up)
        h = jax.nn.silu(gate) * y
        return fp4_linear(h, w_down)

    def _L1_attn_ref(x, w_qkv, w_out):
        import jax, jax.numpy as jnp
        import numpy as np
        DIM = 128
        DIM_HEADS = 64
        b, n, _ = x.shape
        h = DIM_HEADS
        qkv = jnp.einsum('bnc,fc->bnf', x, w_qkv)
        q, k, v = jnp.split(qkv, 3, axis=-1)
        q = q.transpose(0, 2, 1)[..., None]
        k = k.transpose(0, 2, 1)[..., None]
        v = v.transpose(0, 2, 1)[..., None]
        scale = 1.0 / jnp.sqrt(jnp.float32(h))
        dots = jnp.einsum('bhid,bhjd->bhij', q, k) * scale
        causal = jnp.tril(jnp.ones((n, n), dtype=bool))
        dots = jnp.where(causal, dots, -jnp.inf)
        attn = jax.nn.softmax(dots, axis=-1)
        out = jnp.einsum('bhij,bhjd->bhid', attn, v)
        out = out[..., 0].transpose(0, 2, 1)
        return jnp.einsum('bnh,ch->bnc', out, w_out)

    def _L1_xattn_ref(values, keys, query, mask, Wq, Wk, Wv, Wo, bo, num_heads):
        import jax, jax.numpy as jnp
        import numpy as np
        EMBED = 128
        HEADS = 16
        HEAD_DIM = EMBED // HEADS
        B, S = (2, 256)
        WINDOW = 128

        def _sliding_window_mask(seq_len, window_size):
            i = jnp.arange(seq_len)[:, None]
            j = jnp.arange(seq_len)[None, :]
            half = window_size // 2
            allowed = (j >= i - half) & (j <= i + half)
            return jnp.where(allowed, 0.0, -jnp.inf).astype(jnp.float32)
        N, Q, E = query.shape
        H = num_heads
        D = E // H
        v = jnp.einsum('nlhd,ed->nlhe', values.reshape(N, -1, H, D), Wv)
        k = jnp.einsum('nlhd,ed->nlhe', keys.reshape(N, -1, H, D), Wk)
        q = jnp.einsum('nlhd,ed->nlhe', query.reshape(N, -1, H, D), Wq)
        energy = jnp.einsum('nqhd,nkhd->nhqk', q, k)
        window = _sliding_window_mask(Q, WINDOW)[None, None]
        combined = mask + window
        energy = jnp.where(combined == 0, jnp.float32(-1e+20), energy)
        attn = jax.nn.softmax(energy / jnp.sqrt(jnp.float32(E)), axis=-1)
        out = jnp.einsum('nhqk,nkhd->nqhd', attn, v).reshape(N, Q, E)
        return out @ Wo.T + bo

    def _L1_ffn_ref(x, in_proj_w, in_proj_b, out_proj_w, out_proj_b, ln1_g, ln1_b, ln2_g, ln2_b, w_group, b_group, w_expert, b_expert, w1, b1, w2, b2):
        import jax, jax.numpy as jnp
        import numpy as np
        NHEAD = 16
        NUM_GROUPS = 4
        EXPERTS_PER_GROUP = 2
        LN_EPS = 1e-05

        def _layernorm(x, g, b):
            mu = jnp.mean(x, axis=-1, keepdims=True)
            var = jnp.mean(jnp.square(x - mu), axis=-1, keepdims=True)
            return (x - mu) * jax.lax.rsqrt(var + LN_EPS) * g + b

        def _mha(x, wi, bi, wo, bo):
            B, S, D = x.shape
            hd = D // NHEAD
            qkv = x @ wi.T + bi
            q, k, v = jnp.split(qkv, 3, axis=-1)

            def heads(t):
                return t.reshape(B, S, NHEAD, hd).transpose(0, 2, 1, 3)
            q, k, v = (heads(q), heads(k), heads(v))
            scores = jnp.einsum('bhqd,bhkd->bhqk', q, k) / jnp.sqrt(jnp.asarray(hd, x.dtype))
            attn = jax.nn.softmax(scores, axis=-1)
            o = jnp.einsum('bhqk,bhkd->bhqd', attn, v)
            o = o.transpose(0, 2, 1, 3).reshape(B, S, D)
            return o @ wo.T + bo

        def _hier_moe(x, w_group, b_group, w_expert, b_expert, w1, b1, w2, b2):
            B, S, D = x.shape
            xt = x.reshape(B * S, D)
            T = xt.shape[0]
            E = NUM_GROUPS * EXPERTS_PER_GROUP
            gp = jax.nn.softmax(xt @ w_group + b_group, axis=-1)
            g_idx = jnp.argmax(gp, axis=-1)
            g_prob = jnp.max(gp, axis=-1)
            elog = jnp.einsum('td,gde->tge', xt, w_expert) + b_expert
            ep = jax.nn.softmax(elog, axis=-1)
            ep_sel = jnp.take_along_axis(ep, g_idx[:, None, None], axis=1)[:, 0, :]
            e_idx_local = jnp.argmax(ep_sel, axis=-1)
            e_prob = jnp.max(ep_sel, axis=-1)
            flat_e = g_idx * EXPERTS_PER_GROUP + e_idx_local
            combine = jax.nn.one_hot(flat_e, E, dtype=xt.dtype) * (g_prob * e_prob)[:, None]
            h = jax.nn.relu(jnp.einsum('td,edf->etf', xt, w1) + b1[:, None, :])
            y = jnp.einsum('etf,efd->etd', h, w2) + b2[:, None, :]
            out = jnp.einsum('te,etd->td', combine, y)
            return out.reshape(B, S, D)
        attn_out = _mha(x, in_proj_w, in_proj_b, out_proj_w, out_proj_b)
        x = _layernorm(x + attn_out, ln1_g, ln1_b)
        moe_out = _hier_moe(x, w_group, b_group, w_expert, b_expert, w1, b1, w2, b2)
        x = _layernorm(x + moe_out, ln2_g, ln2_b)
        return x
    x = _layernorm(x + _L0_attn_ref(x, L0_attn_Wq, L0_attn_bq, L0_attn_Wk, L0_attn_bk, L0_attn_Wv, L0_attn_bv, L0_attn_Wo, L0_attn_bo, L0_attn_Wpk, L0_attn_bpk, L0_attn_Wpq, L0_attn_bpq, L0_attn_rel_emb), axis=-1)
    x = _layernorm(x + _L0_xattn_ref(x, ctx_1024, ctx_1024), axis=-1)
    x = _layernorm(x + _L0_ffn_ref(x, L0_ffn_w_gate, L0_ffn_w_up, L0_ffn_w_down), axis=-1)
    x = _layernorm(x + _L1_attn_ref(x, L1_attn_w_qkv, L1_attn_w_out), axis=-1)
    x = _layernorm(x + _L1_xattn_ref(ctx_1024, ctx_1024, x, mask_Bx1xSxS2_ff0, L1_xattn_Wq, L1_xattn_Wk, L1_xattn_Wv, L1_xattn_Wo, L1_xattn_bo, 16), axis=-1)
    x = _layernorm(x + _L1_ffn_ref(x, L1_ffn_in_proj_w, L1_ffn_in_proj_b, L1_ffn_out_proj_w, L1_ffn_out_proj_b, L1_ffn_ln1_g, L1_ffn_ln1_b, L1_ffn_ln2_g, L1_ffn_ln2_b, L1_ffn_w_group, L1_ffn_b_group, L1_ffn_w_expert, L1_ffn_b_expert, L1_ffn_w1, L1_ffn_b1, L1_ffn_w2, L1_ffn_b2), axis=-1)
    return x

_drawn_inputs = setup_inputs


def setup_inputs(seed=0):
    import zlib

    import numpy as np

    out = dict(_drawn_inputs(seed))
    spreads = {'L0_attn_bq': (0.0, 0.8),
     'L0_attn_bk': (0.0, 0.8),
     'L0_attn_bv': (0.0, 0.293),
     'L0_attn_bo': (0.0, 0.1),
     'L0_attn_bpk': (0.0, 0.8),
     'L0_attn_bpq': (0.0, 0.8),
     'L1_xattn_bo': (0.0, 0.1),
     'L1_ffn_in_proj_b': (0.0, 0.1),
     'L1_ffn_out_proj_b': (0.0, 0.1),
     'L1_ffn_ln1_g': (1.0, 0.2),
     'L1_ffn_ln1_b': (0.0, 0.1),
     'L1_ffn_ln2_g': (1.0, 0.2),
     'L1_ffn_ln2_b': (0.0, 0.1),
     'L1_ffn_b_group': (0.0, 0.1),
     'L1_ffn_b_expert': (0.0, 0.61),
     'L1_ffn_b1': (0.0, 0.61),
     'L1_ffn_b2': (0.0, 0.423)}
    factors = {'L0_attn_Wq': 8.0,
     'L0_attn_Wk': 8.0,
     'L0_attn_Wv': 5.806,
     'L0_attn_Wpk': 8.0,
     'L0_attn_Wpq': 8.0,
     'L0_attn_rel_emb': 8.0,
     'L0_ffn_w_gate': 4.046,
     'L0_ffn_w_up': 4.14,
     'L0_ffn_w_down': 4.151,
     'L1_attn_w_qkv': 4.471,
     'L1_attn_w_out': 4.687}
    for name, (base, spread) in spreads.items():
        noise = np.random.default_rng([zlib.crc32(name.encode()), seed]).standard_normal(out[name].shape)
        drawn = base * np.exp(spread * noise) if base else spread * noise
        out[name] = jnp.asarray(drawn.astype(out[name].dtype))
    for name, factor in factors.items():
        out[name] = (out[name] * factor).astype(out[name].dtype)
    return out
```

```python
from contextlib import ExitStack

import numpy as np
import concourse.bass as bass
from concourse import mybir

ALU = mybir.AluOpType
ACT = mybir.ActivationFunctionType
F32 = mybir.dt.float32
BF16 = mybir.dt.bfloat16
I32 = mybir.dt.int32
AX = mybir.AxisListType

B, S, D = 16, 128, 128
GB = 4
NG = B // GB
H, DH = 16, 8
C = 64
RG = 4
CR = C // RG
FF = 352
QB = 16
NE, EF = 8, 256
HU = H // 2
CU = 8
CAUSAL = -1.0e30
MASKED = -1.0e20
EPS = 1e-5

FIRST = [("WqT", D), ("WkT", D), ("WvT", D), ("WpkT", D), ("WpqT", D), ("rel", D), ("WoT", D),
         ("bq", 1), ("bk", 1), ("bpk", 1), ("bpq", 1), ("bv", D), ("bo", D),
         ("ident", D), ("anti", D), ("hmask", H), ("ones", D)]
SECOND = [("decay", D), ("window", D),
          ("A_qkT", D), ("A_kqT", D), ("A_vT", C), ("A_oT", D),
          ("X_q", D), ("X_k", D), ("X_v", D), ("X_oT", D), ("X_bo", D),
          ("M_qT", D), ("M_kT", D), ("M_vT", D), ("M_oT", D), ("M_bq", 1), ("M_bk", 1),
          ("M_bv", D), ("M_bo", D), ("ln1g", D), ("ln1b", D), ("ln2g", D), ("ln2b", D),
          ("E_r", 12), ("E_rb", 12), ("E_rank", 4),
          ("E_b1", 2 * NE), ("E_b2", D)]
EXPERTS = [("E_w1", NE * EF), ("E_w2", 2 * NE * D)]

RAW = [("wgate", 3 * D), ("wup", 3 * D), ("wdown", FF)]


def columns(fields):
    at, out = 0, {}
    for name, n in fields:
        out[name] = (at, n)
        at += n
    return out, at


def attention_steps(s):
    n = 2 * GB
    for t in range(n + 4):
        if t < n:
            yield s, "qk", t
        if 0 <= t - 1 < n:
            yield s, "tr", t - 1
        if 0 <= t - 2 < n:
            yield s, "pv", t - 2
        if t >= 4 and t % 2 == 0:
            yield s, "oT", (t - 4) // 2
        if t >= 5 and t % 2:
            yield s, "oP", (t - 5) // 2


def group_steps(stages):
    every = range(GB)
    for s in stages:
        if s != "F":
            yield from ((s, "xT", j) for j in every)
        if s == "L":
            yield from ((s, k, 0) for k in ("q", "k", "v"))
            yield from ((s, "c2p", r) for r in range(8))
            yield from ((s, "p2c", r) for r in range(8))
            yield from attention_steps(s)
        if s in "XM":
            yield from ((s, k, 0) for k in ("q", "k", "v"))
            yield from attention_steps(s)
        if s == "R":
            for k in ("cT", "s", "v", "o"):
                yield from ((s, k, j) for j in every)
        if s == "F":
            for k in ("xT", "gu", "hT", "d"):
                yield from ((s, k, j) for j in every)
        if s == "A":
            yield from ((s, k, 0) for k in ("qk0", "qk1", "v"))
            n = GB * C // CU
            for t in range(n + 1):
                if t < n:
                    yield s, "dots", t
                if t:
                    yield s, "apv", t - 1
            yield from ((s, "oT", j) for j in every)
            yield from ((s, "oP", j) for j in every)
        if s == "E":
            yield from ((s, k, 0) for k in ("rt", "cT"))
            yield from ((s, "h", i) for i in range(2 * NE))
            yield from ((s, "y", j) for j in every)


SETUP = [("setup", "rel", 0), ("setup", "rel", 1), ("setup", "pos", 0), ("setup", "pos", 1)] + \
        [("setup", "gate", i) for i in range(3)] + [("setup", "up", i) for i in range(3)] + \
        [("setup", "down", i) for i in range(3)]


def ring_uses(step):
    s, k, i = step
    if k in ("qk", "c2p", "p2c", "gu", "dots", "y"):
        w = [("W", step)]
        return w + [("P", (s, "b2", i))] if k == "y" else w
    if k == "tr":
        return [("T", (s, "tr", 2 * i)), ("T", (s, "tr", 2 * i + 1))]
    if k == "pv":
        return [("P", step)] if i % 2 == 0 else []
    if k == "apv":
        return [("P", step)] if i % (C // CU) == 0 else []
    return [("T", step)]


class Ring:

    def __init__(self, tiles, full, free, setup, group):
        self.tiles, self.full, self.free = tiles, full, free
        self.at, self.waited = {}, {}
        first = [0, 0]
        for n, key in enumerate(setup):
            self.at[key] = (n % 2, n // 2, 0)
            first[n % 2] += 1
        per = [(len(group) + 1) // 2, len(group) // 2]
        for n, key in enumerate(group):
            self.at[key] = (n % 2, first[n % 2] + n // 2, per[n % 2])

    def tile(self, key):
        return self.tiles[self.at[key][0]]

    def wait(self, eng, g, sem, n, per):
        at = id(eng), id(sem), per
        if n > self.waited.get(at, 0):
            self.waited[at] = n
            eng.wait_ge(sem, g * per + n if per else n)

    def wait_free(self, pe, g, key):
        p, n, per = self.at[key]
        self.wait(pe, g, self.free[p], n + 1, per)

    def wait_full(self, eng, g, key):
        p, n, per = self.at[key]
        self.wait(eng, g, self.full[p], n + 1, per)

    def filled(self, ins, key):
        ins.then_inc(self.full[self.at[key][0]], 1)

    def done(self, ins, key):
        ins.then_inc(self.free[self.at[key][0]], 1)

    def wait_done(self, eng, g, *keys):
        for key in sorted(keys, key=lambda key: -self.at[key][1]):
            p, n, per = self.at[key]
            self.wait(eng, g, self.free[p], n + 2, per)


class Signal:

    def __init__(self, sem, per, unit=1):
        self.sem, self.per, self.unit, self.given = sem, per, unit, 0

    def give(self, ins):
        self.given += 1
        return ins.then_inc(self.sem, self.unit)

    def wait(self, eng, g, n):
        assert 0 < n <= self.per
        eng.wait_ge(self.sem, (g * self.per + n) * self.unit)


def build(nc, t, stages):
    steps = list(group_steps(stages))
    units, first_stage = list(stages), stages[0]
    xin = {s: n for n, s in enumerate(stages)}
    NX = len(stages)

    with ExitStack() as ctx:
        def sb(name, shape, dt=F32):
            return ctx.enter_context(nc.sbuf_tensor(name, shape, dt))

        def sem(name):
            return ctx.enter_context(nc.semaphore(name))

        def ring(name, width):
            tiles = [ctx.enter_context(nc.psum_tensor(f"ps_{name}{i}", [128, width], F32)) for i in range(2)]
            use = [[key for step in ss for r, key in ring_uses(step) if r == name] for ss in (SETUP, steps)]
            return Ring(tiles, [sem(f"{name}{i}_full") for i in range(2)],
                        [sem(f"{name}{i}_free") for i in range(2)], *use)
        W, T, P = ring("W", 1024), ring("T", 512), ring("P", 512)

        c1, n1 = columns(FIRST)
        c2, n2 = columns(SECOND)
        c3, n3 = columns(RAW)
        wt1, wt2 = sb("weights1", [128, n1]), sb("weights2", [128, n2])
        cb = sb("consts_bf16", [128, 2 * D], BF16)
        identb, causal = cb[:, 0:D], cb[:, D:2 * D]

        def w(name, rows=128):
            if name in c1:
                return wt1[0:rows, c1[name][0]:sum(c1[name])]
            return wt2[0:rows, c2[name][0]:sum(c2[name])]
        ident, ones1 = w("ident"), w("ones", 1)

        turns = [sb(f"x_turn{n}", [128, GB, D]) for n in range(2)]
        xs = [sb("x_in", [128, GB, D])] + [turns[n % 2] for n in range(1, NX)] + [sb("x_out", [128, GB, D])]
        if "M" in stages and xin["M"]:
            xs[xin["M"]] = sb("x_last_block", [128, GB, D])
        ctxt = sb("context", [128, GB, D])
        maskt = sb("mask", [128, GB, S])
        ctxT = sb("contextT", [128, GB, S])
        xT = sb("xT", [128, GB, S])
        qT = sb("qT", [128, GB, S])
        kT = sb("kT", [128, GB, S])
        PK = sb("pos_key", [128, 2 * S])
        PQ = sb("pos_query", [128, 2 * S])
        V = sb("values", [128, GB, H, DH + 1])
        V2 = sb("channel_values", [128, GB, C, 2])
        Sb = [sb(f"scores{i}", [128, 1024]) for i in range(2)]
        ET = [sb(f"weightsT{i}", [128, 1024]) for i in range(2)]
        O = sb("heads_out", [128, GB, D])
        OT = sb("heads_outT", [128, GB, S])
        RES = sb("residual", [128, GB, D])
        st = sb("statistics", [128, GB, 16])
        halves = sb("minus_half", [128, 1])
        scal = sb("scaled_biases", [128, 4])
        small = sb("small", [128, 180])
        cmask = sb("score_mask", [128, S])[:]
        routing = sb("routing", [128, 4 * 48])
        logits, ldiff, lexp = (routing[:, 48 * n:48 * n + 48] for n in range(3))
        em, oh = routing[:, 144:160], routing[:, 160:176]
        gm, gm2, gs = (routing[:, 176 + 4 * n:180 + 4 * n] for n in range(3))
        eo = sb("first_expert", [128, GB * NE])[:]
        combine = sb("combine", [128, GB, NE])
        combineT = ET[0][:, 0:512]
        wgT, wuT, wdT = sb("wgateT", [128, FF]), sb("wupT", [128, FF]), sb("wdownT", [128, 3, D])

        Qexp, Kexp, C2P, P2C = (sb(n, [128, GB * H * S]) for n in ("q_by_head", "k_by_head", "c2p", "p2c"))
        qexp4 = Qexp[:].rearrange("p (j h q) -> p j h q", j=GB, h=H)
        kexp4 = Kexp[:].rearrange("p (j h q) -> p j h q", j=GB, h=H)
        qexpb = Qexp[:].rearrange("p (b q) -> p b q", q=S)
        kexpb = Kexp[:].rearrange("p (b q) -> p b q", q=S)
        c2pb = C2P[:].rearrange("p (b q) -> p b q", q=S)
        p2cb = P2C[:].rearrange("p (b q) -> p b q", q=S)
        relT = Kexp[:, 4096:4096 + 2 * D].rearrange("p (i s) -> p i s", i=2)
        raw = Kexp[:, 0:n3]
        f_at = [0]

        def part(n):
            f_at[0] += n
            return Qexp[:, f_at[0] - n:f_at[0]]
        xq, xqT = [part(D) for _ in range(GB)], [part(D) for _ in range(GB)]
        eg, hq, hqT = [part(FF) for _ in range(GB)], [part(FF) for _ in range(GB)], [part(3 * D) for _ in range(GB)]
        f1, f2, f3, f4 = (part(FF) for _ in range(4))
        fsm = part(3 * 24)
        QR = P2C[:, 0:4096].bitcast(BF16)
        KR = P2C[:, 4096:8192].bitcast(BF16)
        QM, Q8, CMX, CMN, AR, KK, KRR = (C2P[:, 512 * i:512 * i + 512] for i in range(7))
        qpart = C2P[:, 3584:3584 + 768].bitcast(BF16).rearrange("p (s f) -> p s f", s=3)
        kpart = C2P[:, 4352:4352 + 768].bitcast(BF16).rearrange("p (s f) -> p s f", s=3)
        c4, n4 = columns(EXPERTS)
        experts = P2C[:, 0:n4]
        ew1, ew2 = (experts[:, c4[n][0]:sum(c4[n])] for n in ("E_w1", "E_w2"))
        HID = C2P[:].rearrange("p (i t) -> p i t", i=2 * NE)

        n_att = sum(s in "LXM" for s in stages)
        loaded3, experts_loaded = sem("raw_loaded"), sem("experts_loaded")
        loaded1, loaded2, loadedb = sem("weights1_loaded"), sem("weights2_loaded"), sem("consts_loaded")
        x_loaded, ctx_loaded, mask_loaded = sem("x_loaded"), sem("context_loaded"), sem("mask_loaded")
        stored = sem("out_stored")
        split_stored, qk_rows_loaded = sem("splits_stored"), sem("qk_rows_loaded")
        sigs = {}

        def signal(name, per, unit=1):
            if per:
                sigs[name] = Signal(sem(name), per, unit)
        n_x = GB * len(stages)
        signal("x_ready", n_x)
        signal("kexp_ready", n_att * GB)
        signal("qexp_ready", GB * ("L" in stages))
        n_two = sum(s in "LX" for s in stages)
        signal("summed", n_two * 2 * GB)
        signal("centred", n_two * 2 * GB)
        signal("probs_ready", n_att * 2 * GB)
        n_ln = sum({"M": 1, "E": 2}.get(s, 1) for s in stages) * GB
        signal("var_ready", n_ln)
        signal("rstd_ready", n_ln)
        if "R" in stages:
            signal("cv_ready", GB)
        if "F" in stages:
            signal("xq_ready", GB)
            signal("eg_ready", GB)
            signal("hq_ready", GB)
            signal("hqT_part", GB)
        if "A" in stages:
            signal("kk_ready", 1)
            signal("ksplit_ready", 1)
            signal("qsplit_ready", 1)
        if "E" in stages:
            signal("logits_ready", 1)
            signal("lexp_ready", 1)
            signal("combine_ready", 1)
        set_bias, set_pext, set_q, set_pool = (
            sem(n) for n in ("biases_scaled", "pos_extended", "w_quantised", "pool_set"))
        dve_chain, pool_chain = sem("dve_chain"), sem("pool_chain")

        def turned(eng, g, s):
            T.wait_done(eng, g, (s, "xT", GB - 2), (s, "xT", GB - 1))

        def order(kind, s, what=None):
            return [x for x in stages if x in kind].index(s)
        qscale = {"L": 1 / np.sqrt(3.0 * DH), "X": 1 / np.sqrt(float(D)), "M": 1 / np.sqrt(float(DH))}
        wnames = {"L": ("WqT", "WkT", "WvT", "WoT", "bv", "bo"), "X": ("X_q", "X_k", "X_v", "X_oT", None, "X_bo"),
                  "M": ("M_qT", "M_kT", "M_vT", "M_oT", "M_bv", "M_bo")}
        bcol = {"L": (scal[:, 0:1], w("bk")), "M": (scal[:, 2:3], w("M_bk"))}

        block = ctx.enter_context(nc.Block())

        @block.sync
        def _(sp):
            sp.dma_start(wt1[:], t["weights1"]).then_inc(loaded1, 16)
            sp.dma_start(raw, t["raw"]).then_inc(loaded3, 16)
            sp.dma_start(cb[:], t["consts_bf16"]).then_inc(loadedb, 16)

            def rows(name, g):
                return t[name].rearrange("b t d -> t b d")[:, bass.ds(g * GB, GB), :]

            def load(g):
                sp.dma_start(xs[0][:], rows("x", g)).then_inc(x_loaded, 16)

            def load_context(g):
                sp.dma_start(ctxt[:], rows("ctx", g)).then_inc(ctx_loaded, 16)

            def load_mask(g):
                sp.dma_start(maskt[:], rows("mask", g)).then_inc(mask_loaded, 16)

            def pass_rows(g):
                sigs["qsplit_ready"].wait(sp, g, 1)
                sp.dma_start(t["q_rows"].rearrange("s r f -> r s f"), qpart[:]).then_inc(split_stored, 16)
                sigs["ksplit_ready"].wait(sp, g, 1)
                sp.dma_start(t["k_rows"].rearrange("s r f -> r s f"), kpart[0:C]).then_inc(split_stored, 16)
                sp.wait_ge(split_stored, (g + 1) * 32)
                q, k = t["q_rows"], t["k_rows"]
                for rg in range(RG):
                    p, c = 32 * rg, CR * rg

                    def put(dst, row, n, src):
                        d = dst[p + row:p + row + n].rearrange("p (c f) -> p c f", c=CR)
                        sp.dma_start(d, src).then_inc(qk_rows_loaded, 16)
                    put(QR, 0, 3, q[0:3, c:c + CR])
                    put(QR, 3, 2, q[0:2, c:c + CR])
                    put(QR, 5, 1, q[0:1, c:c + CR])
                    put(QR, 6, 3, q[0:3, C + c:C + c + CR])
                    for row in range(3):
                        put(KR, row, 1, k[0:1, c:c + CR])
                    for row in range(3, 5):
                        put(KR, row, 1, k[1:2, c:c + CR])
                    put(KR, 5, 1, k[2:3, c:c + CR])
                    put(KR, 6, 3, t["ones_rows"])

            def group(g, more):
                if more:
                    sigs["x_ready"].wait(sp, g, GB)
                    load(g + 1)
                if more and "R" in stages:
                    sigs["x_ready"].wait(sp, g, GB * (xin["R"] + 1))
                    load_context(g + 1)
                if "A" in stages:
                    pass_rows(g)
                if "E" in stages:
                    if "A" in stages:
                        sigs["x_ready"].wait(sp, g, GB * (xin["A"] + 1))
                    sp.dma_start(experts, t["experts"]).then_inc(experts_loaded, 16)
                if more and "X" in stages:
                    sigs["x_ready"].wait(sp, g, GB * (xin["X"] + 1))
                    load_mask(g + 1)
                sigs["x_ready"].wait(sp, g, n_x)
                sp.dma_start(rows("out", g), xs[NX][:]).then_inc(stored, 16)

            sp.sem_inc(stored, 16)
            load(0)
            load_context(0)
            load_mask(0)
            with sp.Fori(0, NG - 1) as g:
                group(g, True)
            group(NG - 1, False)
            sp.wait_ge(stored, 16 * (NG + 1))

        @block.tensor
        def _(pe):
            mm = nc.tensor.matmul

            def fill(g, step):
                s, k, i = step
                x = xs[xin[s]] if s in xin else None
                uses = ring_uses(step)
                if k not in ("tr", "pv", "apv") and s != "setup":
                    for r, key in uses:
                        {"W": W, "T": T, "P": P}[r].wait_free(pe, g, key)
                if s == "setup":
                    T.wait_free(pe, 0, step)
                    o = T.tile(step)
                    if k == "rel":
                        last = mm(o[:, 0:D], lhsT=w("rel"), rhs=w("anti") if i else ident, start=True, stop=True)
                    elif k == "pos":
                        T.wait_done(pe, 0, ("setup", "rel", i))
                        last = mm(o[:, 0:D], lhsT=w("WpqT" if i else "WpkT"), rhs=relT[:, i, :], start=True, stop=True)
                    else:
                        pe.wait_ge(set_q, {"gate": i + 1, "up": i + 4, "down": 7}[k])
                        src = {"gate": Sb[0][:, 0:384], "up": Sb[0][:, 512:896], "down": Sb[1][:, 0:FF]}[k]
                        n = min(D, (FF if k == "down" else 3 * D) - D * i)
                        last = pe.transpose(o[0:n, 0:D], src[:, D * i:D * i + n], ident)
                    T.filled(last, step)
                    return
                if k == "xT":
                    o = T.tile(step)
                    if s == "F":
                        sigs["xq_ready"].wait(pe, g, i + 1)
                        last = pe.transpose(o[:, 0:D], xq[i], ident)
                    else:
                        if xin[s] == 0:
                            pe.wait_ge(x_loaded, 16 * (g + 1))
                        else:
                            sigs["x_ready"].wait(pe, g, GB * (xin[s] - 1) + i + 1)
                        last = pe.transpose(o[:, 0:D], x[:, i, :], ident)
                    T.filled(last, step)
                elif k in ("q", "k"):
                    o = T.tile(step)
                    turned(pe, g, s)
                    src = ctxT if (s == "X" and k == "k") else xT
                    T.filled(mm(o[:, 0:512], lhsT=w(wnames[s][0 if k == "q" else 1]), rhs=src[:].rearrange("p j t -> p (j t)"),
                                start=True, stop=True), step)
                elif k == "v" and s != "R":
                    o = T.tile(step)
                    turned(pe, g, s)
                    for j in range(GB):
                        n = C if s == "A" else D
                        src = ctxT if s == "X" else xT
                        rhs, row = (w("A_vT"), None) if s == "A" else (w(wnames[s][2]), wnames[s][4])
                        last = mm(o[:, n * j:n * j + n], lhsT=src[:, j, :], rhs=rhs, start=True, stop=row is None)
                        if row:
                            last = mm(o[:, n * j:n * j + n], lhsT=ones1, rhs=w(row, 1), start=False, stop=True)
                    T.filled(last, step)
                elif k == "c2p":
                    if i == 0:
                        sigs["qexp_ready"].wait(pe, g, GB)
                        pe.wait_ge(set_pext, 2)
                    for n in range(16):
                        q = 16 * i + n
                        last = mm(W.tile(step)[:, 64 * n:64 * n + 64], lhsT=PK[:, S - 1 - q:2 * S - 1 - q],
                                  rhs=qexpb[:, :, q], start=True, stop=True)
                    W.filled(last, step)
                elif k == "p2c":
                    if i == 0:
                        sigs["kexp_ready"].wait(pe, g, GB)
                    for n in range(16):
                        q = 16 * i + n
                        last = mm(W.tile(step)[:, 64 * n:64 * n + 64], lhsT=PQ[:, S - 1 - q:2 * S - 1 - q],
                                  rhs=kexpb[:, :, q], start=True, stop=True)
                    W.filled(last, step)
                elif k == "qk":
                    o, j = W.tile(step), i // 2
                    if i == 0:
                        T.wait_done(pe, g, (s, "q", 0))
                        if s == "L":
                            W.wait_done(pe, g, (s, "c2p", 6), (s, "c2p", 7))
                    sigs["kexp_ready"].wait(pe, g, GB * order("LXM", s) + j + 1)
                    for b in range(2):
                        h0 = HU * (i % 2) + 4 * b
                        last = mm(o[:, 512 * b:512 * b + 512], lhsT=qT[:, j, :],
                                  rhs=kexp4[:, j, h0:h0 + 4, :].rearrange("p h k -> p (h k)"),
                                  start=True, stop=s != "L", skip_group_check=True)
                        if s == "L":
                            for h in range(4):
                                last = mm(o[:, 512 * b + 128 * h:512 * b + 128 * h + 128], lhsT=c2pb[:, H * j + h0 + h, :],
                                          rhs=ident, start=False, stop=h == 3, skip_group_check=True)
                    W.filled(last, step)
                elif k == "tr":
                    sigs["probs_ready"].wait(pe, g, 2 * GB * order("LXM", s) + i + 1)
                    for b in range(2):
                        key = (s, "tr", 2 * i + b)
                        T.wait_free(pe, g, key)
                        for h in range(4):
                            c0 = 512 * b + 128 * h
                            last = pe.transpose(T.tile(key)[:, 128 * h:128 * h + 128], Sb[i % 2][:, c0:c0 + 128], ident)
                        T.filled(last, key)
                elif k == "pv":
                    j, half = i // 2, i % 2
                    key = (s, "pv", 2 * j)
                    if half == 0:
                        P.wait_free(pe, g, key)
                    if i == 0:
                        T.wait_done(pe, g, (s, "v", 0))
                    T.wait_done(pe, g, (s, "tr", 2 * i), (s, "tr", 2 * i + 1))
                    for h in range(HU):
                        hh = HU * half + h
                        last = mm(P.tile(key)[:, 9 * hh:9 * hh + 9], lhsT=ET[i % 2][:, 128 * h:128 * h + 128],
                                  rhs=V[:, j, hh, :], start=True, stop=True)
                    if half:
                        P.filled(last, key)
                elif k == "oT":
                    P.wait_done(pe, g, (s, "apv", (C // CU) * i) if s == "A" else (s, "pv", 2 * i))
                    T.filled(pe.transpose(T.tile(step)[:, 0:D], O[:, i, :], ident), step)
                elif k == "oP":
                    o = T.tile(step)
                    T.wait_done(pe, g, (s, "oT", i))
                    if s == "A":
                        last = mm(o[:, 0:D], lhsT=OT[0:C, i, :], rhs=w("A_oT", C), start=True, stop=True)
                    else:
                        mm(o[:, 0:D], lhsT=OT[:, i, :], rhs=w(wnames[s][3]), start=True, stop=False)
                        last = mm(o[:, 0:D], lhsT=ones1, rhs=w(wnames[s][5], 1), start=False, stop=True)
                    T.filled(last, step)
                elif s == "R":
                    o = T.tile(step)
                    if k == "cT":
                        pe.wait_ge(ctx_loaded, 16 * (g + 1))
                        last = pe.transpose(o[:, 0:D], ctxt[:, i, :], ident)
                    elif k == "s":
                        T.wait_done(pe, g, (s, "cT", i), (s, "xT", i))
                        last = mm(o[:, 0:D], lhsT=ctxT[:, i, :], rhs=xT[:, i, :], start=True, stop=True)
                    elif k == "v":
                        T.wait_done(pe, g, (s, "s", i))
                        last = mm(o[:, 0:1], lhsT=O[:, i, :], rhs=w("ones")[:, 0:1], start=True, stop=True)
                    else:
                        sigs["cv_ready"].wait(pe, g, i + 1)
                        last = mm(o[:, 0:D], lhsT=O[:, i, :], rhs=OT[:, i, :], start=True, stop=True)
                    T.filled(last, step)
                elif s == "F":
                    if k == "gu":
                        o = W.tile(step)
                        T.wait_done(pe, g, (s, "xT", i))
                        mm(o[:, 0:FF], lhsT=xqT[i], rhs=wgT[:], start=True, stop=True)
                        W.filled(mm(o[:, 512:512 + FF], lhsT=xqT[i], rhs=wuT[:], start=True, stop=True), step)
                    elif k == "hT":
                        o = T.tile(step)
                        sigs["hq_ready"].wait(pe, g, i + 1)
                        for b in range(3):
                            n = min(D, FF - D * b)
                            last = pe.transpose(o[0:n, D * b:D * b + D], hq[i][:, D * b:D * b + n], ident)
                        T.filled(last, step)
                    else:
                        o = T.tile(step)
                        sigs["hqT_part"].wait(pe, g, i + 1)
                        T.wait_done(pe, g, (s, "hT", i))
                        for b in range(3):
                            n = min(D, FF - D * b)
                            last = mm(o[:, 0:D], lhsT=hqT[i][0:n, D * b:D * b + D], rhs=wdT[0:n, b, :], start=b == 0, stop=b == 2)
                        T.filled(last, step)
                elif s == "A":
                    if k in ("qk0", "qk1"):
                        turned(pe, g, s)
                        T.filled(mm(T.tile(step)[:, 0:512], lhsT=w("A_qkT" if k == "qk0" else "A_kqT"),
                                    rhs=xT[:].rearrange("p j t -> p (j t)"), start=True, stop=True), step)
                    elif k == "dots":
                        j, c0 = i // (C // CU), CU * (i % (C // CU))
                        o = W.tile(step)
                        if i == 0:
                            pe.wait_ge(qk_rows_loaded, 16 * 11 * RG * (g + 1))
                            pe.wait_ge(loadedb, 16)
                        for b in range(2):
                            mm(o[:, 512 * b:512 * b + 512], lhsT=causal, rhs=identb.unsqueeze(1).to_broadcast([128, 4, 128]),
                               start=True, stop=False, skip_group_check=True)
                            for n in range(4):
                                c = c0 + 4 * b + n
                                p, f = 32 * (c // CR), 512 * (c % CR) + 128 * j
                                last = mm(o[:, 512 * b + 128 * n:512 * b + 128 * n + 128], lhsT=KR[p:p + 9, f:f + 128],
                                          rhs=QR[p:p + 9, f:f + 128], start=False, stop=n == 3, skip_group_check=True)
                        W.filled(last, step)
                    else:
                        j, c0 = i // (C // CU), CU * (i % (C // CU))
                        key = ("A", "apv", (C // CU) * j)
                        if c0 == 0:
                            P.wait_free(pe, g, key)
                        if i == 0:
                            T.wait_done(pe, g, (s, "v", 0))
                        W.wait_done(pe, g, (s, "dots", i))
                        for n in range(CU):
                            c = c0 + n
                            last = mm(P.tile(key)[:, 2 * c:2 * c + 2], lhsT=Sb[i % 2][:, 128 * n:128 * n + 128],
                                      rhs=V2[:, j, c, :], start=True, stop=True)
                        if c0 + CU == C:
                            P.filled(last, key)
                elif s == "E":
                    if k == "rt":
                        o = T.tile(step)
                        turned(pe, g, s)
                        for j in range(GB):
                            mm(o[:, 12 * j:12 * j + 12], lhsT=xT[:, j, :], rhs=w("E_r"), start=True, stop=False)
                            last = mm(o[:, 12 * j:12 * j + 12], lhsT=ones1, rhs=w("E_rb", 1), start=False, stop=True)
                        T.filled(last, step)
                    elif k == "cT":
                        o = T.tile(step)
                        sigs["combine_ready"].wait(pe, g, 1)
                        for j in range(GB):
                            last = pe.transpose(o[0:NE, 128 * j:128 * j + 128], combine[:, j, :], ident)
                        T.filled(last, step)
                    elif k == "h":
                        if i == 0:
                            pe.wait_ge(experts_loaded, 16 * (g + 1))
                        T.filled(mm(T.tile(step)[:, 0:512], lhsT=ew1[:, 128 * i:128 * i + 128],
                                    rhs=xT[:].rearrange("p j t -> p (j t)"), start=True, stop=True), step)
                    else:
                        o, key = W.tile(step), ("E", "b2", i)
                        if i == 0:
                            T.wait_done(pe, g, (s, "h", 2 * NE - 2), (s, "h", 2 * NE - 1), (s, "cT", 0))
                        P.filled(mm(P.tile(key)[:, 0:D], lhsT=combineT[0:NE, 128 * i:128 * i + 128], rhs=w("E_b2", NE),
                                    start=True, stop=True), key)
                        for e in range(NE):
                            for b in range(2):
                                f = 2 * e + b
                                last = mm(o[:, D * e:D * e + D], lhsT=HID[:, f, 128 * i:128 * i + 128],
                                          rhs=ew2[:, D * f:D * f + D], start=b == 0, stop=b == 1)
                        W.filled(last, step)

            for ring in (W, T, P):
                for p in range(2):
                    pe.sem_inc(ring.free[p], 1)
            pe.wait_ge(loaded1, 16)
            for step in SETUP:
                fill(0, step)
            T.wait_done(pe, 0, *SETUP[-2:])
            pe.wait_ge(loaded2, 16)
            with pe.Fori(0, NG) as g:
                for step in steps:
                    fill(g, step)

        @block.scalar
        def _(act):
            A = nc.scalar.activation
            act.dma_start(wt2[:], t["weights2"]).then_inc(loaded2, 16)

            def take(g, step):
                s, k, i = step
                if s == "setup":
                    if k == "rel":
                        T.wait_full(act, 0, step)
                        ins = nc.scalar.copy(relT[:, i, :], T.tile(step)[:, 0:D])
                        T.done(ins, step)
                    if k in ("gate", "up", "down"):
                        T.wait_full(act, 0, step)
                        o = T.tile(step)
                        n = min(D, FF - D * i)
                        if k == "down":
                            ins = nc.scalar.copy(wdT[0:n, i, :], o[0:n, 0:D])
                        else:
                            ins = nc.scalar.copy((wgT if k == "gate" else wuT)[:, D * i:D * i + n], o[:, 0:n])
                        T.done(ins, step)
                    return
                if k == "xT":
                    T.wait_full(act, g, step)
                    ins = nc.scalar.copy(xqT[i] if s == "F" else xT[:, i, :], T.tile(step)[:, 0:D])
                    T.done(ins, step)
                elif k in ("q", "k"):
                    T.wait_full(act, g, step)
                    o = T.tile(step)[:, 0:512]
                    if g is not None and k == "q" and s != "X":
                        act.wait_ge(set_bias, 2)
                    dst = (qT if k == "q" else kT)[:].rearrange("p j t -> p (j t)")
                    if s == "X":
                        ins = A(dst, o, ACT.Copy, scale=float(qscale[s]) if k == "q" else 1.0)
                    else:
                        ins = A(dst, o, ACT.Identity, bias=bcol[s][0 if k == "q" else 1],
                                scale=float(qscale[s]) if k == "q" else 1.0)
                    T.done(ins, step)
                elif k == "v" and s != "R":
                    T.wait_full(act, g, step)
                    if s == "A":
                        ins = nc.scalar.copy(V2[:, :, :, 0], T.tile(step)[:, 0:GB * C].rearrange("p (j c) -> p j c", j=GB))
                    else:
                        ins = nc.scalar.copy(V[:, :, :, 0:DH], T.tile(step)[:, 0:GB * D].rearrange("p (j h d) -> p j h d", j=GB, h=H))
                    T.done(ins, step)
                elif k == "c2p":
                    W.wait_full(act, g, step)
                    ins = nc.scalar.copy(c2pb[:, :, 16 * i:16 * i + 16], W.tile(step)[:].rearrange("p (q b) -> p b q", q=16))
                    W.done(ins, step)
                elif k == "qk":
                    if s == "M":
                        W.wait_done(act, g, step)
                    else:
                        sigs["centred"].wait(act, g, 2 * GB * order("LX", s) + i + 1)
                    sigs["probs_ready"].give(A(Sb[i % 2][:], Sb[i % 2][:], ACT.Exp))
                elif k == "tr":
                    for b in range(2):
                        key = (s, "tr", 2 * i + b)
                        T.wait_full(act, g, key)
                        ins = nc.scalar.copy(ET[i % 2][:, 512 * b:512 * b + 512], T.tile(key)[:])
                        T.done(ins, key)
                elif k == "oT":
                    n = C if s == "A" else D
                    T.wait_full(act, g, step)
                    ins = nc.scalar.copy(OT[0:n, i, :], T.tile(step)[0:n, 0:D])
                    T.done(ins, step)
                elif s == "R" and k == "cT":
                    T.wait_full(act, g, step)
                    ins = nc.scalar.copy(ctxT[:, i, :], T.tile(step)[:, 0:D])
                    T.done(ins, step)
                elif s == "F" and k == "gu":
                    W.wait_full(act, g, step)
                    sigs["eg_ready"].give(A(eg[i], W.tile(step)[:, 0:FF], ACT.Exp, scale=-1.0))
                elif s == "F" and k == "hT":
                    T.wait_full(act, g, step)
                    o = T.tile(step)
                    sigs["hqT_part"].give(nc.scalar.copy(hqT[i][:, 0:2 * D], o[:, 0:2 * D]))
                    n = FF - 2 * D
                    ins = nc.scalar.copy(hqT[i][0:n, 2 * D:3 * D], o[0:n, 2 * D:3 * D])
                    T.done(ins, step)
                elif k == "dots":
                    W.wait_full(act, g, step)
                    ins = A(Sb[i % 2][:], W.tile(step)[:], ACT.Exp)
                    W.done(ins, step)
                elif s == "E" and k == "rt":
                    sigs["logits_ready"].wait(act, g, 1)
                    sigs["lexp_ready"].give(A(lexp, ldiff, ACT.Exp))
                elif s == "E" and k == "cT":
                    T.wait_full(act, g, step)
                    ins = nc.scalar.copy(combineT[0:NE, :], T.tile(step)[0:NE, :])
                    T.done(ins, step)
                elif k == "h":
                    T.wait_full(act, g, step)
                    ins = A(HID[:, i, :], T.tile(step)[:], ACT.Relu, bias=w("E_b1")[:, i:i + 1])
                    T.done(ins, step)

            for step in SETUP:
                take(None, step)
            act.wait_ge(loaded2, 16)
            act.wait_ge(loaded1, 16)
            act.wait_ge(set_pool, 4)
            with act.Fori(0, NG) as g:
                for step in steps:
                    take(g, step)

        @block.gpsimd
        def _(pool):
            nc.gpsimd.memset(halves[:], -0.5).then_inc(set_pool, 1)
            nc.gpsimd.memset(V[:], 1.0).then_inc(set_pool, 1)
            nc.gpsimd.memset(V2[:], 1.0).then_inc(set_pool, 1)
            nc.gpsimd.memset(O[:], 0.0).then_inc(set_pool, 1)
            pool.wait_ge(loaded1, 16)
            pool.wait_ge(set_pool, 4)

            def root(g, n):
                sigs["var_ready"].wait(pool, g, n + 1)
                j = n % GB
                sigs["rstd_ready"].give(nc.gpsimd.tensor_tensor(st[:, j, 9:10], st[:, j, 8:9], halves[:], ALU.pow))

            ln = [0]

            def help_(g, step):
                s, k, i = step
                if s == "L" and k == "q":
                    T.wait_done(pool, g, step)
                    for j in range(GB):
                        sigs["qexp_ready"].give(nc.gpsimd.tensor_tensor(
                            qexp4[:, j], qT[:, j, :].unsqueeze(1).to_broadcast([128, H, S]),
                            w("hmask").unsqueeze(2).to_broadcast([128, H, S]), ALU.mult))
                if k == "qk" and s in "LX":
                    n = 2 * GB * order("LX", s) + i
                    sigs["summed"].wait(pool, g, n + 1)
                    v = Sb[i % 2][:].rearrange("p (h k) -> p h k", h=HU)
                    sigs["centred"].give(nc.gpsimd.tensor_tensor(
                        v, v, small[:, 8 * (i % 2):8 * (i % 2) + 8].unsqueeze(2).to_broadcast([128, HU, S]), ALU.subtract))
                if s == "A" and k == "qk1":
                    sigs["kk_ready"].wait(pool, g, 1)

                    def link(ins):
                        chain[0] += 1
                        ins.then_inc(pool_chain, 1)
                        pool.wait_ge(pool_chain, g * 4 + chain[0])
                    chain = [0]
                    kk, kr, onec = KK[0:C], KRR[0:C], w("ones", C)[:, 0:1].to_broadcast([C, GB * S])
                    link(nc.gpsimd.tensor_tensor(kpart[0:C, 0], kk, onec, ALU.mult))
                    link(nc.gpsimd.tensor_tensor(kr, kk, kpart[0:C, 0], ALU.subtract))
                    link(nc.gpsimd.tensor_tensor(kpart[0:C, 1], kr, onec, ALU.mult))
                    link(nc.gpsimd.tensor_tensor(kr, kr, kpart[0:C, 1], ALU.subtract))
                    sigs["ksplit_ready"].give(nc.gpsimd.tensor_tensor(kpart[0:C, 2], kr, onec, ALU.mult))
                if k == "oP" or (s, k) in (("R", "o"), ("F", "d")):
                    root(g, ln[0])
                    ln[0] += 1
                if (s, k) == ("E", "y"):
                    root(g, ln[0])
                    ln[0] += 1

            with pool.Fori(0, NG) as g:
                for step in steps:
                    help_(g, step)
                if "E" in stages:
                    for j in range(GB):
                        root(g, ln[0])
                        ln[0] += 1

        @block.vector
        def _(dve):
            v = nc.vector
            chain = [0]

            def link(ins):
                chain[0] += 1
                ins.then_inc(dve_chain, 1)
                dve.wait_ge(dve_chain, chain[0])

            def quantise(dst, src, n, give=None):
                nb = n // QB
                a, r1, t1, q1 = (x[:, 0:n] for x in (f1, f2, f3, f4))
                amax, sc, rs = (fsm[:, 24 * i:24 * i + nb] for i in range(3))

                def blocks(x):
                    return x.rearrange("p (b q) -> p b q", q=QB)

                def spread(x):
                    return x.unsqueeze(2).to_broadcast([128, nb, QB])
                link(v.tensor_reduce(amax, blocks(src), AX.X, ALU.max, apply_absolute_value=True))
                link(v.tensor_scalar(sc, amax, 1.0 / 6.0, 1e-12, ALU.mult, ALU.max))
                link(v.reciprocal(rs, sc))
                link(v.tensor_tensor(blocks(q1), blocks(src), spread(rs), ALU.mult))
                link(v.tensor_scalar(a.bitcast(I32), q1.bitcast(I32), 0x7FFFFFFF, None, ALU.bitwise_and))
                link(v.tensor_scalar(t1, a, 5.0, 2.0, ALU.is_gt, ALU.mult))
                link(v.tensor_scalar(r1, a, 1.75, None, ALU.is_gt))
                link(v.scalar_tensor_tensor(t1, a, 3.5, t1, ALU.is_gt, ALU.add))
                link(v.scalar_tensor_tensor(r1, a, 1.25, r1, ALU.is_gt, ALU.add))
                link(v.scalar_tensor_tensor(t1, a, 2.5, t1, ALU.is_gt, ALU.add))
                link(v.scalar_tensor_tensor(r1, a, 0.75, r1, ALU.is_gt, ALU.add))
                link(v.scalar_tensor_tensor(r1, a, 0.25, r1, ALU.is_gt, ALU.add))
                link(v.scalar_tensor_tensor(r1, r1, 0.5, t1, ALU.mult, ALU.add))
                link(v.tensor_tensor(blocks(a), blocks(r1), spread(sc), ALU.mult))
                link(v.tensor_scalar(t1.bitcast(I32), src.bitcast(I32), -2 ** 31, None, ALU.bitwise_and))
                give(v.tensor_tensor(dst.bitcast(I32), a.bitcast(I32), t1.bitcast(I32), ALU.bitwise_or))

            n_ln_done = [0]

            def normalise(g, j, res, out, gain=None, give=None):
                link(v.bn_stats(st[:, j, 0:6], res))
                link(v.bn_aggr(st[:, j, 6:8], st[:, j, 0:6]))
                ins = v.tensor_scalar(st[:, j, 8:9], st[:, j, 7:8], EPS, None, ALU.add)
                n_ln_done[0] += 1
                sigs["var_ready"].give(ins)
                sigs["rstd_ready"].wait(dve, g, n_ln_done[0])
                dst = out if gain is None else res
                ins = v.tensor_scalar(dst, res, st[:, j, 6:7], st[:, j, 9:10], ALU.subtract, ALU.mult)
                if gain:
                    link(ins)
                    link(v.tensor_tensor(res, res, w(gain + "g"), ALU.mult))
                    ins = v.tensor_tensor(out, res, w(gain + "b"), ALU.add)
                if give:
                    give(ins)
                else:
                    link(ins)

            def x_out(s):
                return sigs["x_ready"].give

            def setup():
                dve.wait_ge(loaded1, 16)
                dve.wait_ge(loaded2, 16)
                dve.wait_ge(set_pool, 4)
                v.tensor_scalar(scal[:, 0:1], w("bq"), float(qscale["L"]), None, ALU.mult).then_inc(set_bias, 1)
                v.tensor_scalar(scal[:, 2:3], w("M_bq"), float(qscale["M"]), None, ALU.mult).then_inc(set_bias, 1)
                for i, dst in enumerate((PK, PQ)):
                    step = ("setup", "pos", i)
                    T.wait_full(dve, 0, step)
                    ins = v.tensor_scalar(dst[:, 63:191] if i == 0 else dst[:, 64:192], T.tile(step)[:, 0:D],
                                          w("bpq" if i else "bpk"), float(qscale["L"]) if i else 1.0, ALU.add, ALU.mult)
                    T.done(ins, step)
                    T.wait_done(dve, 0, step)
                    lo = 63 if i == 0 else 64
                    link(v.tensor_copy(dst[:, 0:lo], dst[:, lo:lo + 1].to_broadcast([128, lo])))
                    hi = lo + D
                    v.tensor_copy(dst[:, hi:2 * S], dst[:, hi - 1:hi].to_broadcast([128, 2 * S - hi])).then_inc(set_pext, 1)
                dve.wait_ge(loaded3, 16)
                for name, buf in (("wgate", Sb[0][:, 0:384]), ("wup", Sb[0][:, 512:896])):
                    for i in range(3):
                        quantise(buf[:, D * i:D * i + D], raw[:, c3[name][0] + D * i:c3[name][0] + D * i + D], D, lambda ins: ins.then_inc(set_q, 1))
                quantise(Sb[1][:, 0:FF], raw[:, c3["wdown"][0]:n3], FF, lambda ins: ins.then_inc(set_q, 1))

            def work(g, step):
                s, k, i = step
                if s in "LXM" and k == "k":
                    T.wait_done(dve, g, step)
                    for j in range(GB):
                        sigs["kexp_ready"].give(v.tensor_tensor(
                            kexp4[:, j], kT[:, j, :].unsqueeze(1).to_broadcast([128, H, S]),
                            w("hmask").unsqueeze(2).to_broadcast([128, H, S]), ALU.mult))
                elif k == "p2c":
                    W.wait_full(dve, g, step)
                    ins = v.tensor_copy(p2cb[:, :, 16 * i:16 * i + 16], W.tile(step)[:].rearrange("p (q b) -> p b q", q=16))
                    W.done(ins, step)
                    W.wait_done(dve, g, step)
                elif k == "qk" and s in "LXM":
                    j, h0 = i // 2, HU * (i % 2)
                    if s == "X" and i % 2 == 0:
                        if i == 0:
                            dve.wait_ge(mask_loaded, 16 * (g + 1))
                        link(v.scalar_tensor_tensor(cmask, maskt[:, j, :], 0.0, w("window"), ALU.is_equal, ALU.mult))
                    W.wait_full(dve, g, step)
                    sc = Sb[i % 2][:].rearrange("p (h k) -> p h k", h=HU)
                    ps = W.tile(step)[:].rearrange("p (h k) -> p h k", h=HU)
                    mx = small[:, 8 * (i % 2):8 * (i % 2) + 8]
                    if s == "M":
                        link(v.tensor_reduce(mx, ps, AX.X, ALU.max))
                        ins = v.tensor_tensor(sc, ps, mx.unsqueeze(2).to_broadcast([128, HU, S]), ALU.subtract)
                        W.done(ins, step)
                    else:
                        add = p2cb[:, H * j + h0:H * j + h0 + HU, :] if s == "L" else \
                            cmask.unsqueeze(1).to_broadcast([128, HU, S])
                        ins = v.tensor_tensor(sc, ps, add, ALU.add)
                        W.done(ins, step)
                        W.wait_done(dve, g, step)
                        sigs["summed"].give(v.tensor_reduce(mx, sc, AX.X, ALU.max))
                elif k == "pv" and i % 2:
                    j, key = i // 2, (s, "pv", i - 1)
                    P.wait_full(dve, g, key)
                    o = P.tile(key)[:, 0:9 * H].rearrange("p (h d) -> p h d", h=H)
                    r = small[:, 16 + 16 * (j % 2):32 + 16 * (j % 2)].unsqueeze(2)
                    link(v.reciprocal(r, o[:, :, DH:DH + 1]))
                    ins = v.tensor_tensor(O[:, j, :].rearrange("p (h d) -> p h d", h=H), o[:, :, 0:DH],
                                          r.to_broadcast([128, H, DH]), ALU.mult)
                    P.done(ins, key)
                elif k == "apv" and i % (C // CU) == C // CU - 1:
                    j = i // (C // CU)
                    key = (s, "apv", (C // CU) * j)
                    P.wait_full(dve, g, key)
                    o = P.tile(key)[:, 0:2 * C].rearrange("p (c d) -> p c d", c=C)
                    r = small[:, 48 + C * (j % 2):48 + C + C * (j % 2)].unsqueeze(2)
                    link(v.reciprocal(r, o[:, :, 1:2]))
                    ins = v.tensor_tensor(O[:, j, 0:C].unsqueeze(2), o[:, :, 0:1], r, ALU.mult)
                    P.done(ins, key)
                elif k == "oP" or (s, k) in (("R", "o"), ("F", "d")):
                    T.wait_full(dve, g, step)
                    if xin[s] == 0:
                        dve.wait_ge(x_loaded, 16 * (g + 1))
                    ins = v.tensor_tensor(RES[:, i, :], T.tile(step)[:, 0:D], xs[xin[s]][:, i, :], ALU.add)
                    T.done(ins, step)
                    T.wait_done(dve, g, step)
                    if xin[s] + 1 == NX and i == 0:
                        dve.wait_ge(stored, 16 * g + 16)
                    normalise(g, i, RES[:, i, :], xs[xin[s] + 1][:, i, :], "ln1" if s == "M" else None, x_out(s))
                elif s == "R" and k == "s":
                    T.wait_full(dve, g, step)
                    ins = v.tensor_tensor(O[:, i, :], T.tile(step)[:, 0:D], w("decay"), ALU.mult)
                    T.done(ins, step)
                elif s == "R" and k == "v":
                    T.wait_full(dve, g, step)
                    r = small[:, 176 + i:177 + i]
                    link(v.tensor_scalar(r, T.tile(step)[:, 0:1], -1.0, 1.0, ALU.mult, ALU.max))
                    ins = v.tensor_tensor(r, T.tile(step)[:, 0:1], r, ALU.max)
                    T.done(ins, step)
                    T.wait_done(dve, g, step)
                    link(v.reciprocal(r, r))
                    sigs["cv_ready"].give(v.tensor_scalar(OT[:, i, :], ctxt[:, i, :], r, None, ALU.mult))
                elif s == "F" and k == "xT":
                    if i == 0 and xin[s] == 0:
                        dve.wait_ge(x_loaded, 16 * (g + 1))
                    if xin[s]:
                        sigs["x_ready"].wait(dve, g, GB * (xin[s] - 1) + i + 1)
                    quantise(xq[i], xs[xin[s]][:, i, :], D, sigs["xq_ready"].give)
                elif s == "F" and k == "gu":
                    o = W.tile(step)
                    sigs["eg_ready"].wait(dve, g, i + 1)
                    W.wait_full(dve, g, step)
                    if i:
                        sigs["hq_ready"].wait(dve, g, i)
                    link(v.tensor_scalar(f1, eg[i], 1.0, None, ALU.add))
                    link(v.reciprocal(f1, f1))
                    link(v.tensor_tensor(f1, f1, o[:, 0:FF], ALU.mult))
                    ins = v.tensor_tensor(eg[i], f1, o[:, 512:512 + FF], ALU.mult)
                    W.done(ins, step)
                    W.wait_done(dve, g, step)
                    quantise(hq[i], eg[i], FF, sigs["hq_ready"].give)
                elif s == "A" and k == "qk0":
                    T.wait_full(dve, g, step)
                    o = T.tile(step)
                    link(v.tensor_scalar(QM[0:C], o[0:C], 0.125, None, ALU.mult))
                    ins = v.tensor_copy(KK[C:2 * C], o[C:2 * C])
                    T.done(ins, step)
                    T.wait_done(dve, g, step)
                elif s == "A" and k == "qk1":
                    T.wait_full(dve, g, step)
                    o = T.tile(step)
                    sigs["kk_ready"].give(v.tensor_copy(KK[0:C], o[0:C]))
                    ins = v.tensor_scalar(Q8[C:2 * C], o[C:2 * C], 0.125, None, ALU.mult)
                    T.done(ins, step)
                    T.wait_done(dve, g, step)
                    for j in range(GB):
                        f = slice(128 * j, 128 * j + 128)
                        kj = KK[C:2 * C, f]
                        link(v.tensor_tensor_scan(CMX[C:2 * C, f], kj, kj, -3.0e38, ALU.max, ALU.max))
                        link(v.tensor_tensor_scan(CMN[C:2 * C, f], kj, kj, 3.0e38, ALU.min, ALU.min))
                    hi = slice(C, 2 * C)
                    link(v.scalar_tensor_tensor(CMX[hi], Q8[hi], -1.0, CMX[hi], ALU.mult, ALU.mult))
                    link(v.scalar_tensor_tensor(CMN[hi], Q8[hi], -1.0, CMN[hi], ALU.mult, ALU.mult))
                    link(v.tensor_tensor(QM[hi], CMX[hi], CMN[hi], ALU.min))
                    link(v.tensor_copy(qpart[:, 0], QM))
                    link(v.tensor_tensor(AR, QM, qpart[:, 0], ALU.subtract))
                    link(v.tensor_copy(qpart[:, 1], AR))
                    link(v.tensor_tensor(AR, AR, qpart[:, 1], ALU.subtract))
                    sigs["qsplit_ready"].give(v.tensor_copy(qpart[:, 2], AR))
                elif s == "E" and k == "rt":
                    T.wait_full(dve, g, step)
                    ins = v.tensor_copy(logits, T.tile(step)[:, 0:48])
                    T.done(ins, step)
                    T.wait_done(dve, g, step)
                    L = logits.rearrange("p (j n) -> p j n", j=GB)
                    Dl = ldiff.rearrange("p (j n) -> p j n", j=GB)
                    le = L[:, :, 4:12].rearrange("p j (g e) -> p j g e", e=2)
                    de = Dl[:, :, 4:12].rearrange("p j (g e) -> p j g e", e=2)
                    em4 = em.rearrange("p (j n) -> p j n", j=GB)
                    link(v.tensor_reduce(gm, L[:, :, 0:4], AX.X, ALU.max))
                    link(v.tensor_tensor(Dl[:, :, 0:4], L[:, :, 0:4], gm.unsqueeze(2).to_broadcast([128, GB, 4]), ALU.subtract))
                    link(v.tensor_tensor(em4, le[:, :, :, 0], le[:, :, :, 1], ALU.max))
                    link(v.tensor_tensor(de[:, :, :, 0], le[:, :, :, 0], em4, ALU.subtract))
                    sigs["logits_ready"].give(v.tensor_tensor(de[:, :, :, 1], le[:, :, :, 1], em4, ALU.subtract))
                    oh4 = oh.rearrange("p (j n) -> p j n", j=GB)
                    EO = eo.rearrange("p (j g e) -> p j g e", j=GB, e=2)
                    link(v.tensor_tensor(oh4, L[:, :, 0:4], gm.unsqueeze(2).to_broadcast([128, GB, 4]), ALU.is_equal))
                    link(v.tensor_tensor(oh4, oh4, w("E_rank").unsqueeze(1).to_broadcast([128, GB, 4]), ALU.mult))
                    link(v.tensor_reduce(gm2, oh4, AX.X, ALU.max))
                    link(v.tensor_tensor(oh4, oh4, gm2.unsqueeze(2).to_broadcast([128, GB, 4]), ALU.is_equal))
                    link(v.tensor_tensor(EO[:, :, :, 0], le[:, :, :, 0], le[:, :, :, 1], ALU.is_ge))
                    link(v.tensor_scalar(EO[:, :, :, 1], EO[:, :, :, 0], -1.0, 1.0, ALU.mult, ALU.add))
                    sigs["lexp_ready"].wait(dve, g, 1)
                    X = lexp.rearrange("p (j n) -> p j n", j=GB)
                    xe = X[:, :, 4:12].rearrange("p j (g e) -> p j g e", e=2)
                    link(v.tensor_reduce(gs, X[:, :, 0:4], AX.X, ALU.add))
                    link(v.tensor_tensor(em4, xe[:, :, :, 0], xe[:, :, :, 1], ALU.add))
                    link(v.reciprocal(gs, gs))
                    link(v.reciprocal(em, em))
                    link(v.tensor_tensor(em4, em4, gs.unsqueeze(2).to_broadcast([128, GB, 4]), ALU.mult))
                    link(v.tensor_tensor(em4, em4, oh4, ALU.mult))
                    cm = combine.rearrange("p j (g e) -> p j g e", e=2)
                    link(v.tensor_tensor(cm[:, :, :, 0], EO[:, :, :, 0], em4, ALU.mult))
                    ins = v.tensor_tensor(cm[:, :, :, 1], EO[:, :, :, 1], em4, ALU.mult)
                    sigs["combine_ready"].give(ins)
                    sigs["combine_ready"].wait(dve, g, 1)
                elif s == "E" and k == "y":
                    res, key = RES[:, i, :], ("E", "b2", i)
                    P.wait_full(dve, g, key)
                    ins = v.tensor_tensor(res, P.tile(key)[:, 0:D], xs[xin[s]][:, i, :], ALU.add)
                    P.done(ins, key)
                    P.wait_done(dve, g, key)
                    W.wait_full(dve, g, step)
                    for e in range(NE):
                        ins = v.scalar_tensor_tensor(res, W.tile(step)[:, D * e:D * e + D], combine[:, i, e:e + 1], res,
                                                     ALU.mult, ALU.add)
                        if e < NE - 1:
                            link(ins)
                    W.done(ins, step)
                    W.wait_done(dve, g, step)
                    normalise(g, i, res, O[:, i, :], "ln2")

            def finish(g):
                for j in range(GB):
                    link(v.tensor_tensor(RES[:, j, :], O[:, j, :], xs[xin["M"]][:, j, :], ALU.add))
                    if j == 0:
                        dve.wait_ge(stored, 16 * g + 16)
                    normalise(g, j, RES[:, j, :], xs[NX][:, j, :], None, sigs["x_ready"].give)

            setup()
            last_setup = chain[0]
            with dve.Fori(0, NG) as g:
                dve.sem_clear(dve_chain)
                chain[0] = 0
                for step in steps:
                    work(g, step)
                if "E" in stages:
                    finish(g)

        for name, x in sigs.items():
            assert x.given == x.per, (name, x.given, x.per)


def shape_constants():
    at = np.arange(S)
    out = {"ident": np.eye(D), "anti": np.eye(D)[::-1], "ones": np.ones((128, D)),
           "hmask": (at[:, None] // DH == np.arange(H)[None, :]), "E_rank": np.tile(np.arange(4, 0, -1), (128, 1)),
           "window": np.where(abs(at[:, None] - at[None, :]) <= 64, MASKED / np.sqrt(float(D)), 0.0)}
    dm = np.where(at[:, None] >= at[None, :], 0.96875 ** (at[None, :] - at[:, None]).astype(np.float64), 0.0)
    dm = dm / np.sqrt(dm.sum(axis=1)) / np.sqrt(float(D))
    out["decay"] = dm.T
    return {n: a.astype(np.float32) for n, a in out.items()}


STAGES = "LRFAXME"


def kernel(**inputs):
    import ml_dtypes
    import concourse.bacc as bacc
    from concourse.bass_utils import run_bass_kernel_spmd

    a = {n: np.asarray(x) for n, x in inputs.items()}
    f32 = np.float32

    def pack(fields, parts):
        at, n = columns(fields)
        out = np.zeros((128, n), f32)
        for name, (c, width) in at.items():
            x = parts[name]
            x = x.reshape(-1, 1) if x.ndim == 1 and width == 1 else np.atleast_2d(x)
            assert x.shape[1] == width, name
            out[0:x.shape[0], c:c + width] = x
        return out

    def rows3(x):
        out = np.zeros((3 * 128, D), f32)
        out[0:x.shape[0]] = x
        return out.reshape(3, 128, D).transpose(1, 0, 2).reshape(128, 3 * D)

    def by_head(x):
        out = np.zeros((D, D), f32)
        for h in range(H):
            out[DH * h:DH * h + DH, DH * h:DH * h + DH] = x.T
        return out

    def wide(x):
        return np.broadcast_to(x, (128, D))
    p = {n: x for n, x in shape_constants().items()}
    for n in ("Wq", "Wk", "Wv", "Wpk", "Wpq", "Wo"):
        p[n + "T"] = a["L0_attn_" + n].T
    for n in ("bq", "bk", "bpk", "bpq", "bv", "bo"):
        p[n] = a["L0_attn_" + n]
    p["rel"] = a["L0_attn_rel_emb"]
    p["wgate"], p["wup"], p["wdown"] = rows3(a["L0_ffn_w_gate"]), rows3(a["L0_ffn_w_up"]), a["L0_ffn_w_down"]
    wq, wk, wv = (a["L1_attn_w_qkv"][C * n:C * n + C].T for n in range(3))
    p["A_qkT"], p["A_kqT"], p["A_vT"] = np.concatenate([wq, wk], 1), np.concatenate([wk, wq], 1), wv
    p["A_oT"] = a["L1_attn_w_out"].T
    p["X_q"], p["X_k"], p["X_v"] = (by_head(a["L1_xattn_" + n]) for n in ("Wq", "Wk", "Wv"))
    p["X_oT"], p["X_bo"] = a["L1_xattn_Wo"].T, a["L1_xattn_bo"]
    e = "L1_ffn_"
    p["M_qT"], p["M_kT"], p["M_vT"] = (a[e + "in_proj_w"][D * n:D * n + D].T for n in range(3))
    p["M_bq"], p["M_bk"], p["M_bv"] = (a[e + "in_proj_b"][D * n:D * n + D] for n in range(3))
    p["M_oT"], p["M_bo"] = a[e + "out_proj_w"].T, a[e + "out_proj_b"]
    for n in ("ln1_g", "ln1_b", "ln2_g", "ln2_b"):
        p[n.replace("_", "")] = wide(a[e + n])
    p["E_r"] = np.concatenate([a[e + "w_group"], a[e + "w_expert"].transpose(1, 0, 2).reshape(D, NE)], 1)
    p["E_rb"] = np.concatenate([a[e + "b_group"], a[e + "b_expert"].reshape(NE)])
    p["E_w1"] = a[e + "w1"].transpose(1, 0, 2).reshape(D, NE * EF)
    p["E_b1"] = a[e + "b1"].reshape(2 * NE, 128).T
    p["E_w2"] = a[e + "w2"].reshape(2 * NE, 128, D).transpose(1, 0, 2).reshape(128, 2 * NE * D)
    p["E_b2"] = a[e + "b2"]

    bf = ml_dtypes.bfloat16
    at = np.arange(S)
    consts = np.concatenate([np.eye(D), np.where(at[None, :] > at[:, None], CAUSAL, 0.0)], 1).astype(bf)
    arrays = {"weights1": pack(FIRST, p), "weights2": pack(SECOND, p), "consts_bf16": consts, "raw": pack(RAW, p),
              "experts": pack(EXPERTS, p),
              "ones_rows": np.ones((3, CR, GB * S), bf),
              "x": np.ascontiguousarray(a["x"]), "ctx": np.ascontiguousarray(a["ctx_1024"]),
              "mask": np.ascontiguousarray(a["mask_Bx1xSxS2_ff0"].reshape(B, S, S))}
    nc = bacc.Bacc("TRN2", target_bir_lowering=False, num_devices=1)
    t = {n: nc.dram_tensor("in_" + n, x.shape, mybir.dt.from_np(x.dtype), kind="ExternalInput").ap() for n, x in arrays.items()}
    t["out"] = nc.dram_tensor("out_0", (B, S, D), F32, kind="ExternalOutput").ap()
    t["q_rows"] = nc.dram_tensor("q_rows", (3, 2 * C, GB * S), BF16).ap()
    t["k_rows"] = nc.dram_tensor("k_rows", (3, C, GB * S), BF16).ap()
    build(nc, t, STAGES)
    r = run_bass_kernel_spmd(nc, [{"in_" + n: x for n, x in arrays.items()}], core_ids=[0])
    return r.results[0]["out_0"]
```

```python
from contextlib import ExitStack

import numpy as np
import concourse.bass as bass
from concourse import mybir

ALU = mybir.AluOpType
ACT = mybir.ActivationFunctionType
F32 = mybir.dt.float32
BF16 = mybir.dt.bfloat16
I32 = mybir.dt.int32
AX = mybir.AxisListType

B, S, D = 16, 128, 128
GB = 4
NG = B // GB
NH = 2
JH = GB // NH
H, DH = 16, 8
C = 64
RG = 4
CR = C // RG
FF = 352
QB = 16
NE, EF = 8, 256
HU = H // 2
UH = 2 * JH
CU = 8
US = C // CU
QD = C // 4
PAIRS = [(0, 0), (1, 0), (2, 0), (0, 1), (1, 1), (0, 2)]
ROWS = len(PAIRS) + 3
CAUSAL = -1.0e30
MASKED = -1.0e20
EPS = 1e-5

FIRST = [("WqT", D), ("WkT", D), ("WvT", D), ("WpkT", D), ("WpqT", D), ("rel", D), ("WoT", D),
         ("bq", 1), ("bk", 1), ("bpk", 1), ("bpq", 1), ("bv", D), ("bo", D),
         ("ident", D), ("anti", D), ("hmask", H), ("ones", D), ("qmask", QD * QD), ("smask", 4)]
SECOND = [("decay", D), ("window", D),
          ("A_qkT", D), ("A_kqT", D), ("A_vT", C), ("A_oT", D),
          ("X_q", D), ("X_k", D), ("X_v", D), ("X_oT", D), ("X_bo", D),
          ("M_qT", D), ("M_kT", D), ("M_vT", D), ("M_oT", D), ("M_bq", 1), ("M_bk", 1),
          ("M_bv", D), ("M_bo", D), ("ln1g", D), ("ln1b", D), ("ln2g", D), ("ln2b", D),
          ("E_r", 12), ("E_rb", 12), ("E_rank", 4),
          ("E_b1", 2 * NE), ("E_b2", D)]
EXPERTS = [("E_w1", NE * EF), ("E_w2", 2 * NE * D)]

RAW = [("wgate", 3 * D), ("wup", 3 * D), ("wdown", FF)]


def columns(fields):
    at, out = 0, {}
    for name, n in fields:
        out[name] = (at, n)
        at += n
    return out, at


def group_work(stages):
    work = []

    def add(step, cost, *after):
        work.append((step, cost, after))
    for n, s in enumerate(stages):
        for h in range(NH):
            mine = range(JH * h, JH * h + JH)
            queries = [((s, "q", x), 0.0) for x in range(NH)] if s == "L" else []
            for j in mine:
                before = [((stages[n - 1],) + LAST[stages[n - 1]] + (x,), 5.5 if s == "F" else 0.5)
                          for x in (mine if s == "F" else [j]) if n]
                if s == "F" and j > mine[0]:
                    before.append(((s, "xT", j - 1), 0.0))
                add((s, "xT", j), 0.25, *before)
                if s == "R":
                    add((s, "cT", j), 0.25)
            turned = [((s, "xT", j), 1.0) for j in mine]
            if s in "LXM":
                free = [(("A", "apv", US * (JH * h + JH) - 1), 0.5)] if s == "X" and "A" in stages else []
                add((s, "k", h), 0.5, *(free if s == "X" else turned), *queries)
                add((s, "v", h), 0.9 if s == "X" else 1.8, *(free if s == "X" else turned), *queries)
                add((s, "q", h), 0.5, *turned)
            if s == "L" and h == NH - 1:
                for k, x in (("c2p", "q"), ("p2c", "k")):
                    for r in range(8):
                        before = ((s, k, r - 1) if r else (s, "c2p", 7), 0.0)
                        add((s, k, r), 6.9, *[((s, x, half), 5.0) for half in range(NH)],
                            *([before] if r or k == "p2c" else []))
            if s == "A":
                add((s, "qk0", h), 0.5, *turned)
                add((s, "qk1", h), 0.5, *turned, ((s, "qk0", h), 0.0))
                add((s, "v", h), 0.5, *turned, ((s, "qk1", h), 0.0))
    for n, s in enumerate(stages):
        for h in range(NH):
            mine = range(JH * h, JH * h + JH)
            if s in "LXM":
                for i in range(UH * h, UH * h + UH):
                    j = i // 2
                    before = [((s, "qk", i - 1), 0.0)] if i % UH else []
                    add((s, "qk", i), 5.1 if s == "L" else 1.7, ((s, "k", h), 0.5), ((s, "q", h), 1.0),
                        *before, *([((s, "p2c", 7), 1.5)] if s == "L" else []))
                    add((s, "tr", i), 1.7, ((s, "qk", i), 1.7 if s == "M" else 3.7))
                    before = [((s, "pv", i - 1), 2.0 if i % 2 == 0 else 0.0)] if i % UH else []
                    add((s, "pv", i), 3.4, ((s, "tr", i), 1.3), ((s, "v", h), 1.0), *before)
                    if i % 2:
                        add((s, "oT", j), 0.25, ((s, "pv", i), 0.4))
                        add((s, "oP", j), 0.9, ((s, "oT", j), 0.8))
            if s == "R":
                for j in mine:
                    add((s, "s", j), 0.45, ((s, "xT", j), 0.8), ((s, "cT", j), 0.8))
                    add((s, "v", j), 0.45, ((s, "s", j), 0.4))
                    add((s, "o", j), 0.45, ((s, "v", j), 0.4))
            if s == "F":
                for j in mine:
                    before = [((s, "gu", j - 1), 0.0)] if j > mine[0] else []
                    add((s, "gu", j), 1.3, ((s, "xT", j), 0.8), *before)
                for j in mine:
                    add((s, "hT", j), 0.7, ((s, "gu", mine[-1]), 1.5))
                    add((s, "d", j), 1.3, ((s, "hT", j), 1.5))
            if s == "A":
                for i in range(US * JH * h, US * JH * (h + 1)):
                    j = i // US
                    before = [((s, "dots", i - 1), 0.0)] if i % (US * JH) else []
                    add((s, "dots", i), 1.3, ((s, "qk0", h), 16.0), ((s, "qk1", h), 16.0), *before)
                    before = [((s, "apv", i - 1), 2.0 if i % US == 0 else 0.0)] if i % (US * JH) else []
                    add((s, "apv", i), 1.7, ((s, "dots", i), 1.6), ((s, "v", h), 5.0), *before)
                    if i % US == US - 1:
                        add((s, "nT", j), 0.25, ((s, "apv", i), 0.4))
                        add((s, "oT", j), 0.25, ((s, "nT", j), 0.5))
                        add((s, "oP", j), 0.45, ((s, "oT", j), 0.8))
            if s == "E":
                turned = [((s, "xT", j), 1.0) for j in mine]
                add((s, "rt", h), 1.7, *turned)
                add((s, "cT", h), 0.5, ((s, "rt", h), 2.0))
                for f in range(2 * NE):
                    before = [((s, "h", 2 * NE * h + f - 1), 0.0)] if f else []
                    add((s, "h", 2 * NE * h + f), 0.45, *turned, *before)
                last = 2 * NE * (h + 1) - 1
                for j in mine:
                    add((s, "y", j), 7.0, ((s, "h", last), 1.0), ((s, "cT", h), 1.0))
                    add((s, "end", j), 0.0, ((s, "y", j), 0.0))
    return work


BEHIND = (0.0, 6.0, 35.0, 43.0)
HASTE = {"L": -14.5, "R": 1.2, "F": -10.3, "A": 0.0, "X": 0.0, "M": -9.4, "E": 0.0}

LAST = {"L": ("oP",), "R": ("o",), "F": ("d",), "A": ("oP",), "X": ("oP",), "M": ("oP",), "E": ("end",)}


def vector_cost(step):
    s, k, i = step
    if k == "v" and s != "R":
        return 0.0
    if k == "k":
        return 5.0
    if k == "oP" or (s, k) in (("R", "o"), ("F", "d")):
        return 3.2 if s == "M" else 2.6
    return {"p2c": 1.3, "qk": 2.5, "qk0": 1.0, "qk1": 5.0, "nT": 0.4, "s": 0.3, "v": 0.7, "rt": 5.0, "y": 5.3,
            "gu": 2.0 + 12.0 * (i % JH == JH - 1),
            "end": 2.8, "pv": 0.7 * (i % 2), "apv": 1.0 * (i % US == US - 1)}.get(k, 0.0)


def sequence(step):
    s, k, i = step
    if k in ("c2p", "p2c"):
        return 0
    if k in ("qk", "tr", "pv"):
        return i // 2
    if k in ("dots", "apv"):
        return i // US
    if k == "h":
        return JH * (i // (2 * NE))
    halves = k in ("q", "k", "qk0", "qk1", "rt") or (k == "v" and s != "R") or (s, k) == ("E", "cT")
    return JH * i if halves else i


def buffered(steps):
    units = [(s, i) for s, k, i in steps if k in ("qk", "dots")]
    turns = [(s, i) for s, k, i in steps if k == "tr"]
    return {u: n % 2 for n, u in enumerate(units)}, {u: n % 2 for n, u in enumerate(turns)}


def group_steps(stages):
    work = group_work(stages)
    cost = {step: c for step, c, after in work}
    after = {step: a for step, c, a in work}
    follow = {step: [] for step in cost}
    for step, c, a in work:
        for x, lag in a:
            follow[x].append((step, lag))
    way = {}

    def way_to_end(step):
        if step not in way:
            way[step] = cost[step] + vector_cost(step) + max([lag + way_to_end(x) for x, lag in follow[step]], default=0.0)
        return way[step]
    order, ended, now, vector = [], {}, 0.0, 0.0
    left = sorted(cost, key=lambda step: BEHIND[sequence(step)] + HASTE[step[0]] * sequence(step) - way_to_end(step))
    scores, weights = [], []

    def room(step):
        s, k, i = step
        if k in ("qk", "dots"):
            n = len(scores)
            return n < 2 or (scores[n - 2][0], "apv" if scores[n - 2][0] == "A" else "tr", scores[n - 2][1]) in ended
        n = len(weights)
        return k != "tr" or n < 2 or (weights[n - 2][0], "pv", weights[n - 2][1]) in ended
    while left:
        able = [x for x in left if all(a in ended for a, lag in after[x]) and room(x)]
        when = {x: max([ended[a] + lag for a, lag in after[x]], default=0.0) for x in able}
        now = max(now, min(when.values()))
        step = next(x for x in able if when[x] <= now)
        now += cost[step]
        if vector_cost(step):
            vector = max(vector, now) + vector_cost(step)
        ended[step] = vector if vector_cost(step) else now
        order.append(step)
        left.remove(step)
        if step[1] in ("qk", "dots"):
            scores.append((step[0], step[2]))
        if step[1] == "tr":
            weights.append((step[0], step[2]))
    return order


SETUP = [("setup", "rel", 0), ("setup", "rel", 1), ("setup", "pos", 0), ("setup", "pos", 1)] + \
        [("setup", "gate", i) for i in range(3)] + [("setup", "up", i) for i in range(3)] + \
        [("setup", "down", i) for i in range(3)]


def ring_uses(step):
    s, k, i = step
    if k in ("qk", "c2p", "p2c", "gu", "dots", "y"):
        w = [("W", step)]
        return w + [("P", (s, "b2", i))] if k == "y" else w
    if k == "tr":
        return [("T", (s, "tr", 2 * i)), ("T", (s, "tr", 2 * i + 1))]
    if k == "pv":
        return [("P", step)] if i % 2 == 0 else []
    if k == "apv":
        return [("P", step)] if i % US == 0 else []
    if k == "end":
        return []
    return [("T", step)]


def half_of(key):
    s, k, i = key
    return i // {"pv": UH, "apv": US * JH, "b2": JH}[k]


class Ring:

    def __init__(self, tiles, full, free, setup, group, choose=None):
        self.tiles, self.full, self.free = tiles, full, free
        self.waited = {}
        first, per, at = [0, 0], [0, 0], {}
        for n, key in enumerate(setup):
            at[key] = (n % 2, first[n % 2])
            first[n % 2] += 1
        self.at = {key: (p, n, 0) for key, (p, n) in at.items()}
        at = {}
        for n, key in enumerate(group):
            p = choose(key) if choose else n % 2
            at[key] = (p, first[p] + per[p])
            per[p] += 1
        self.at.update({key: (p, n, per[p]) for key, (p, n) in at.items()})

    def tile(self, key):
        return self.tiles[self.at[key][0]]

    def due(self, eng, sem, g, n, per):
        at = id(eng), id(sem), per
        if n > self.waited.get(at, 0):
            self.waited[at] = n
            yield sem, g * per + n if per else n

    def emptied(self, pe, g, key):
        p, n, per = self.at[key]
        return self.due(pe, self.free[p], g, n + 1, per)

    def filled(self, eng, g, key):
        p, n, per = self.at[key]
        return self.due(eng, self.full[p], g, n + 1, per)

    def taken(self, eng, g, *keys):
        for key in sorted(keys, key=lambda key: -self.at[key][1]):
            p, n, per = self.at[key]
            yield from self.due(eng, self.free[p], g, n + 2, per)

    def full_of(self, key):
        return self.full[self.at[key][0]]

    def free_of(self, key):
        return self.free[self.at[key][0]]


class Signal:

    def __init__(self, sem, keys):
        self.sem, self.keys, self.given = sem, list(keys), 0
        self.at = {key: n + 1 for n, key in enumerate(self.keys)}

    def next(self, key):
        assert self.keys[self.given] == key, (self.keys[self.given], key)
        self.given += 1
        return self.sem

    def count(self, g, *keys):
        return self.sem, g * len(self.keys) + max(self.at[key] for key in keys)


def build(nc, t, stages):
    steps = group_steps(stages)
    score_of, weight_of = buffered(steps)
    xin = {s: n for n, s in enumerate(stages)}
    NX = len(stages)

    with ExitStack() as ctx:
        def sb(name, shape, dt=F32):
            return ctx.enter_context(nc.sbuf_tensor(name, shape, dt))

        def sem(name):
            return ctx.enter_context(nc.semaphore(name))

        def ring(name, width):
            tiles = [ctx.enter_context(nc.psum_tensor(f"ps_{name}{i}", [128, width], F32)) for i in range(2)]
            use = [[key for step in ss for r, key in ring_uses(step) if r == name] for ss in (SETUP, steps)]
            return Ring(tiles, [sem(f"{name}{i}_full") for i in range(2)],
                        [sem(f"{name}{i}_free") for i in range(2)], *use, half_of if name == "P" else None)
        W, T, P = ring("W", 1024), ring("T", 512), ring("P", 512)

        c1, n1 = columns(FIRST)
        c2, n2 = columns(SECOND)
        c3, n3 = columns(RAW)
        wt1, wt2 = sb("weights1", [128, n1]), sb("weights2", [128, n2])
        cb = sb("consts_bf16", [128, 2 * D], BF16)
        identb, causal = cb[:, 0:D], cb[:, D:2 * D]

        def w(name, rows=128):
            if name in c1:
                return wt1[0:rows, c1[name][0]:sum(c1[name])]
            return wt2[0:rows, c2[name][0]:sum(c2[name])]
        ident, ones1 = w("ident"), w("ones", 1)

        turns = [sb(f"x_turn{n}", [128, GB, D]) for n in range(2)]
        xs = [sb("x_in", [128, GB, D])] + [turns[n % 2] for n in range(1, NX)] + [sb("x_out", [128, GB, D])]
        if "M" in stages and xin["M"]:
            xs[xin["M"]] = sb("x_last_block", [128, GB, D])
        ctxt = sb("context", [128, GB, D])
        maskt = sb("mask", [128, GB, S])
        ctxT = sb("contextT", [128, GB, S])
        xT = sb("xT", [128, GB, S])
        qT = sb("qT", [128, GB, S])
        kT = sb("kT", [128, GB, S])
        PK = sb("pos_key", [128, 2 * S])
        PQ = sb("pos_query", [128, 2 * S])
        V = sb("values", [128, GB, H, DH + 1])
        VA = sb("channel_values", [128, GB, C])
        Sb = [sb(f"scores{i}", [128, 1024]) for i in range(2)]
        ET = [sb(f"weightsT{i}", [128, 1024]) for i in range(2)]
        O = sb("heads_out", [128, GB, D])
        OT = sb("heads_outT", [128, GB, S])
        RES = sb("residual", [128, GB, D])
        st = sb("statistics", [128, GB, 16])
        halves = sb("minus_half", [128, 1])
        scal = sb("scaled_biases", [128, 4])
        small = sb("small", [128, 16 + (H + C + 1) * GB])
        cmasks = sb("score_masks", [128, NH, S])
        routing = sb("routing", [128, 4 * 48])
        logits, ldiff, lexp = (routing[:, 48 * n:48 * n + 12 * JH] for n in range(3))
        em, oh = routing[:, 144:144 + 4 * JH], routing[:, 160:160 + 4 * JH]
        gm, gm2, gs = (routing[:, 176 + 4 * n:176 + 4 * n + JH] for n in range(3))
        eo = sb("first_expert", [128, JH * NE])[:]
        combine = sb("combine", [128, GB, NE])
        combineT = sb("combineT", [NE, GB * S])
        wgT, wuT, wdT = sb("wgateT", [128, FF]), sb("wupT", [128, FF]), sb("wdownT", [128, 3, D])

        Qexp, Kexp, C2P, P2C = (sb(n, [128, GB * H * S]) for n in ("q_by_head", "k_by_head", "c2p", "p2c"))
        qexp4 = Qexp[:].rearrange("p (j h q) -> p j h q", j=GB, h=H)
        kexp4 = Kexp[:].rearrange("p (j h q) -> p j h q", j=GB, h=H)
        qexpb = Qexp[:].rearrange("p (b q) -> p b q", q=S)
        kexpb = Kexp[:].rearrange("p (b q) -> p b q", q=S)
        c2pb = C2P[:].rearrange("p (b q) -> p b q", q=S)
        p2cb = P2C[:].rearrange("p (b q) -> p b q", q=S)
        relT = Kexp[:, 4096:4096 + 2 * D].rearrange("p (i s) -> p i s", i=2)
        raw = Kexp[:, 0:n3]
        f_at = [0]

        def part(n):
            f_at[0] += n
            return Qexp[:, f_at[0] - n:f_at[0]]
        RH = GB * H * S // NH
        xq, eg, hq = ([part(JH * n) for _ in range(NH)] for n in (D, FF, FF))
        xqT, hqT = ([part(n) for _ in range(GB)] for n in (D, 3 * D))
        f1, f2, f3, f4 = (part(JH * FF) for _ in range(4))
        fsm = sb("block_scales", [128, 3 * JH * FF // QB])[:]
        QR = [P2C[:, RH * h:RH * h + RH // 2].bitcast(BF16) for h in range(NH)]
        KR = [P2C[:, RH * h + RH // 2:RH * h + RH].bitcast(BF16) for h in range(NH)]
        n = JH * S
        asplit = [[C2P[:, RH * h + n * i:RH * h + n * i + n] for i in range(7)] for h in range(NH)]

        def parts(h, at):
            at += RH * h
            return C2P[:, at:at + 3 * n // 2].bitcast(BF16).rearrange("p (s f) -> p s f", s=3)
        qpart, kpart = [parts(h, 7 * n) for h in range(NH)], [parts(h, 9 * n) for h in range(NH)]
        VZ = Kexp[:].rearrange("p (j q c) -> p j q c", j=GB, q=QD)
        c4, n4 = columns(EXPERTS)
        experts = Qexp[:, 0:n4]
        ew1, ew2 = (experts[:, c4[n][0]:sum(c4[n])] for n in ("E_w1", "E_w2"))
        HID = [C2P[:, RH * h:RH * h + RH].rearrange("p (i t) -> p i t", i=2 * NE) for h in range(NH)]

        loaded3, experts_loaded = sem("raw_loaded"), sem("experts_loaded")
        loaded1, loaded2, loadedb = sem("weights1_loaded"), sem("weights2_loaded"), sem("consts_loaded")
        x_loaded, ctx_loaded, mask_loaded = sem("x_loaded"), sem("context_loaded"), sem("mask_loaded")
        stored = sem("out_stored")
        split_stored = sem("splits_stored")
        qk_rows_loaded = [sem(f"qk_rows{h}_loaded") for h in range(NH)]
        sigs = {}

        def each(*kinds, of=stages):
            return [(s, i) for s, k, i in steps if k in kinds and s in of]

        def signal(name, keys):
            if keys:
                sigs[name] = Signal(sem(name), keys)
        outputs = [(s, i) for s, k, i in steps if (k,) == LAST[s]]
        first_out = [x for x in outputs if x[0] == stages[-1]][0]
        signal("x_ready", outputs)
        signal("kexp_ready", [(s, j) for s, h in each("k") for j in range(JH * h, JH * h + JH)])
        signal("qexp_ready", each("q", of="L")[:1])
        signal("qexp_late_ready", each("q", of="L")[1:])
        signal("summed", each("qk", of="LX"))
        signal("centred", each("qk", of="LX"))
        signal("probs_ready", each("qk"))
        norms = [(s, k, i) for s, k, i in steps if (k,) == LAST[s] or k == "y"]
        signal("var_ready", norms)
        signal("rstd_ready", norms)
        signal("cv_ready", each("v", of="R"))
        first_of = [(s, i // JH) for s, i in each("xT", of="F") if i % JH == 0]
        signal("xq_ready", first_of)
        signal("eg_ready", each("gu"))
        last_of = [(s, i // JH) for s, i in each("gu") if i % JH == JH - 1]
        signal("hq_ready", last_of)
        signal("hqT_part", each("hT"))
        signal("kk_ready", each("qk1"))
        signal("ksplit_ready", each("qk1"))
        signal("qsplit_ready", each("qk1"))
        spread = [(s, j) for s, h in each("v", of="A") for j in range(JH * h, JH * h + JH)]
        signal("ones_spread", spread)
        signal("values_spread", spread)
        signal("logits_ready", each("rt"))
        signal("lexp_ready", each("rt"))
        signal("combine_ready", each("rt"))
        set_bias, set_pext, set_q, set_pool = (
            sem(n) for n in ("biases_scaled", "pos_extended", "w_quantised", "pool_set"))
        dve_chain, pool_chain = sem("dve_chain"), sem("pool_chain")

        def turned(eng, g, s, h, k="xT"):
            for due in T.taken(eng, g, *[(s, k, j) for j in range(JH * h, JH * h + JH)]):
                eng.wait_ge(*due)

        def half(x, h):
            return x[:, JH * h:JH * h + JH, :]
        qscale = {"L": 1 / np.sqrt(3.0 * DH), "X": 1 / np.sqrt(float(D)), "M": 1 / np.sqrt(float(DH))}
        wnames = {"L": ("WqT", "WkT", "WvT", "WoT", "bv", "bo"), "X": ("X_q", "X_k", "X_v", "X_oT", None, "X_bo"),
                  "M": ("M_qT", "M_kT", "M_vT", "M_oT", "M_bv", "M_bo")}
        bcol = {"L": (scal[:, 0:1], w("bk")), "M": (scal[:, 2:3], w("M_bk"))}

        q_halves = [h for s, h in each("q", of="L")]

        def spread_queries(engine, j):
            return engine.tensor_tensor(qexp4[:, j], qT[:, j, :].unsqueeze(1).to_broadcast([128, H, S]),
                                        w("hmask").unsqueeze(2).to_broadcast([128, H, S]), ALU.mult)

        block = ctx.enter_context(nc.Block())

        @block.sync
        def _(sp):
            sp.dma_start(wt1[:], t["weights1"]).then_inc(loaded1, 16)
            sp.dma_start(raw, t["raw"]).then_inc(loaded3, 16)
            sp.dma_start(cb[:], t["consts_bf16"]).then_inc(loadedb, 16)

            def rows(name, g):
                return t[name].rearrange("b t d -> t b d")[:, bass.ds(g * GB, GB), :]

            def load(g):
                sp.dma_start(xs[0][:], rows("x", g)).then_inc(x_loaded, 16)

            def load_context(g):
                sp.dma_start(ctxt[:], rows("ctx", g)).then_inc(ctx_loaded, 16)

            def load_mask(g):
                sp.dma_start(maskt[:], rows("mask", g)).then_inc(mask_loaded, 16)

            def pass_rows(g, h):
                q, k = t["q_rows"][h], t["k_rows"][h]
                sp.wait_ge(*sigs["qsplit_ready"].count(g, ("A", h)))
                sp.dma_start(q.rearrange("s r f -> r s f"), qpart[h][:]).then_inc(split_stored, 16)
                sp.wait_ge(*sigs["ksplit_ready"].count(g, ("A", h)))
                sp.dma_start(k.rearrange("s r f -> r s f"), kpart[h][0:C]).then_inc(split_stored, 16)
                sp.wait_ge(split_stored, g * 32 * NH + 32 * (h_order.index(h) + 1))

                def put(dst, row, src):
                    sp.dma_start(dst[row:128:32], src).then_inc(qk_rows_loaded[h], 16)
                q = q.rearrange("s (r c) f -> r s (c f)", c=CR)
                k = k.rearrange("s (r c) f -> r s (c f)", c=CR)
                for row, (a, b) in enumerate(PAIRS):
                    put(QR[h], row, q[0:RG, a])
                    put(KR[h], row, k[:, b])
                for a in range(3):
                    put(QR[h], len(PAIRS) + a, q[RG:2 * RG, a])
                    put(KR[h], len(PAIRS) + a, t["ones_rows"])

            def all_of(s):
                return [(s, j) for j in range(GB)]
            h_order = [h for s, h in each("qk1")]

            def group(g, more):
                for h in h_order:
                    pass_rows(g, h)
                if more:
                    sp.wait_ge(*sigs["x_ready"].count(g, *all_of(stages[0])))
                    load(g + 1)
                if more and "R" in stages:
                    sp.wait_ge(*sigs["x_ready"].count(g, *all_of("R")))
                    load_context(g + 1)
                if "E" in stages:
                    sp.wait_ge(*sigs["x_ready"].count(g, *[x for x in outputs if x[0] in stages[0] + "LF"]))
                    sp.dma_start(experts, t["experts"]).then_inc(experts_loaded, 16)
                if more and "X" in stages:
                    sp.wait_ge(*sigs["x_ready"].count(g, *all_of("X")))
                    load_mask(g + 1)
                sp.wait_ge(*sigs["x_ready"].count(g, outputs[-1]))
                sp.dma_start(rows("out", g), xs[NX][:]).then_inc(stored, 16)

            sp.sem_inc(stored, 16)
            load(0)
            load_context(0)
            load_mask(0)
            with sp.Fori(0, NG - 1) as g:
                group(g, True)
            group(NG - 1, False)
            sp.wait_ge(stored, 16 * (NG + 1))

        @block.tensor
        def _(pe):
            mm = nc.tensor.matmul

            def fill(g, step):
                s, k, i = step
                x = xs[xin[s]] if s in xin else None
                uses = ring_uses(step)
                if k not in ("tr", "pv", "apv") and s != "setup":
                    for r, key in uses:
                        for due in {"W": W, "T": T, "P": P}[r].emptied(pe, g, key):
                            pe.wait_ge(*due)
                if s == "setup":
                    for due in T.emptied(pe, 0, step):
                        pe.wait_ge(*due)
                    o = T.tile(step)
                    if k == "rel":
                        last = mm(o[:, 0:D], lhsT=w("rel"), rhs=w("anti") if i else ident, start=True, stop=True)
                    elif k == "pos":
                        for due in T.taken(pe, 0, ("setup", "rel", i)):
                            pe.wait_ge(*due)
                        last = mm(o[:, 0:D], lhsT=w("WpqT" if i else "WpkT"), rhs=relT[:, i, :], start=True, stop=True)
                    else:
                        pe.wait_ge(set_q, {"gate": i + 1, "up": i + 4, "down": 7}[k])
                        src = {"gate": Sb[0][:, 0:384], "up": Sb[0][:, 512:896], "down": Sb[1][:, 0:FF]}[k]
                        n = min(D, (FF if k == "down" else 3 * D) - D * i)
                        last = pe.transpose(o[0:n, 0:D], src[:, D * i:D * i + n], ident)
                    last.then_inc(T.full_of(step), 1)
                    return
                if k == "xT":
                    o = T.tile(step)
                    if s == "F":
                        pe.wait_ge(*sigs["xq_ready"].count(g, (s, i // JH)))
                        last = pe.transpose(o[:, 0:D], xq[i // JH][:, D * (i % JH):D * (i % JH) + D], ident)
                    else:
                        if xin[s] == 0:
                            pe.wait_ge(x_loaded, 16 * (g + 1))
                        else:
                            pe.wait_ge(*sigs["x_ready"].count(g, (stages[xin[s] - 1], i)))
                        last = pe.transpose(o[:, 0:D], x[:, i, :], ident)
                    last.then_inc(T.full_of(step), 1)
                elif k in ("q", "k"):
                    o = T.tile(step)
                    src = ctxT if (s == "X" and k == "k") else xT
                    turned(pe, g, s if src is xT else "R", i, "xT" if src is xT else "cT")
                    mm(o[:, 0:JH * S], lhsT=w(wnames[s][0 if k == "q" else 1]),
                                rhs=half(src, i).rearrange("p j t -> p (j t)"), start=True, stop=True) \
                        .then_inc(T.full_of(step), 1)
                elif k == "v" and s != "R":
                    o = T.tile(step)
                    turned(pe, g, *(("R", i, "cT") if s == "X" else (s, i)))
                    for j in range(JH):
                        n = C if s == "A" else D
                        src = ctxT if s == "X" else xT
                        rhs, row = (w("A_vT"), None) if s == "A" else (w(wnames[s][2]), wnames[s][4])
                        last = mm(o[:, n * j:n * j + n], lhsT=src[:, JH * i + j, :], rhs=rhs, start=True, stop=row is None)
                        if row:
                            last = mm(o[:, n * j:n * j + n], lhsT=ones1, rhs=w(row, 1), start=False, stop=True)
                    last.then_inc(T.full_of(step), 1)
                elif k == "c2p":
                    if i == 0:
                        pe.wait_ge(*sigs["qexp_ready"].count(g, (s, q_halves[0])))
                        pe.wait_ge(*sigs["qexp_late_ready"].count(g, (s, q_halves[1])))
                        pe.wait_ge(set_pext, 2)
                    for n in range(16):
                        q = 16 * i + n
                        last = mm(W.tile(step)[:, 64 * n:64 * n + 64], lhsT=PK[:, S - 1 - q:2 * S - 1 - q],
                                  rhs=qexpb[:, :, q], start=True, stop=True)
                    last.then_inc(W.full_of(step), 1)
                elif k == "p2c":
                    if i == 0:
                        pe.wait_ge(*sigs["kexp_ready"].count(g, *[(s, j) for j in range(GB)]))
                    for n in range(16):
                        q = 16 * i + n
                        last = mm(W.tile(step)[:, 64 * n:64 * n + 64], lhsT=PQ[:, S - 1 - q:2 * S - 1 - q],
                                  rhs=kexpb[:, :, q], start=True, stop=True)
                    last.then_inc(W.full_of(step), 1)
                elif k == "qk":
                    o, j = W.tile(step), i // 2
                    for due in T.taken(pe, g, (s, "q", j // JH)):
                        pe.wait_ge(*due)
                    if s == "L":
                        for due in W.taken(pe, g, (s, "c2p", 6), (s, "c2p", 7)):
                            pe.wait_ge(*due)
                    pe.wait_ge(*sigs["kexp_ready"].count(g, (s, j)))
                    for b in range(2):
                        h0 = HU * (i % 2) + 4 * b
                        last = mm(o[:, 512 * b:512 * b + 512], lhsT=qT[:, j, :],
                                  rhs=kexp4[:, j, h0:h0 + 4, :].rearrange("p h k -> p (h k)"),
                                  start=True, stop=s != "L", skip_group_check=True)
                        if s == "L":
                            for h in range(4):
                                last = mm(o[:, 512 * b + 128 * h:512 * b + 128 * h + 128], lhsT=c2pb[:, H * j + h0 + h, :],
                                          rhs=ident, start=False, stop=h == 3, skip_group_check=True)
                    last.then_inc(W.full_of(step), 1)
                elif k == "tr":
                    pe.wait_ge(*sigs["probs_ready"].count(g, (s, i)))
                    for b in range(2):
                        key = (s, "tr", 2 * i + b)
                        for due in T.emptied(pe, g, key):
                            pe.wait_ge(*due)
                        for h in range(4):
                            c0 = 512 * b + 128 * h
                            last = pe.transpose(T.tile(key)[:, 128 * h:128 * h + 128], Sb[score_of[s, i]][:, c0:c0 + 128], ident)
                        last.then_inc(T.full_of(key), 1)
                elif k == "pv":
                    j, second = i // 2, i % 2
                    key = (s, "pv", 2 * j)
                    if second == 0:
                        for due in P.emptied(pe, g, key):
                            pe.wait_ge(*due)
                    for due in T.taken(pe, g, (s, "v", j // JH)):
                        pe.wait_ge(*due)
                    for due in T.taken(pe, g, (s, "tr", 2 * i), (s, "tr", 2 * i + 1)):
                        pe.wait_ge(*due)
                    for h in range(HU):
                        hh = HU * second + h
                        last = mm(P.tile(key)[:, 9 * hh:9 * hh + 9], lhsT=ET[weight_of[s, i]][:, 128 * h:128 * h + 128],
                                  rhs=V[:, j, hh, :], start=True, stop=True)
                    if second:
                        last.then_inc(P.full_of(key), 1)
                elif k == "oT":
                    if s == "A":
                        for due in T.taken(pe, g, (s, "nT", i)):
                            pe.wait_ge(*due)
                    else:
                        for due in P.taken(pe, g, (s, "pv", 2 * i)):
                            pe.wait_ge(*due)
                    pe.transpose(T.tile(step)[:, 0:D], O[:, i, :], ident).then_inc(T.full_of(step), 1)
                elif k == "oP":
                    o = T.tile(step)
                    for due in T.taken(pe, g, (s, "oT", i)):
                        pe.wait_ge(*due)
                    if s == "A":
                        last = mm(o[:, 0:D], lhsT=OT[0:C, i, :], rhs=w("A_oT", C), start=True, stop=True)
                    else:
                        mm(o[:, 0:D], lhsT=OT[:, i, :], rhs=w(wnames[s][3]), start=True, stop=False)
                        last = mm(o[:, 0:D], lhsT=ones1, rhs=w(wnames[s][5], 1), start=False, stop=True)
                    last.then_inc(T.full_of(step), 1)
                elif s == "R":
                    o = T.tile(step)
                    if k == "cT":
                        pe.wait_ge(ctx_loaded, 16 * (g + 1))
                        last = pe.transpose(o[:, 0:D], ctxt[:, i, :], ident)
                    elif k == "s":
                        for due in T.taken(pe, g, (s, "cT", i), (s, "xT", i)):
                            pe.wait_ge(*due)
                        last = mm(o[:, 0:D], lhsT=ctxT[:, i, :], rhs=xT[:, i, :], start=True, stop=True)
                    elif k == "v":
                        for due in T.taken(pe, g, (s, "s", i)):
                            pe.wait_ge(*due)
                        last = mm(o[:, 0:1], lhsT=O[:, i, :], rhs=w("ones")[:, 0:1], start=True, stop=True)
                    else:
                        pe.wait_ge(*sigs["cv_ready"].count(g, (s, i)))
                        last = mm(o[:, 0:D], lhsT=O[:, i, :], rhs=OT[:, i, :], start=True, stop=True)
                    last.then_inc(T.full_of(step), 1)
                elif s == "F":
                    if k == "gu":
                        o = W.tile(step)
                        for due in T.taken(pe, g, (s, "xT", i)):
                            pe.wait_ge(*due)
                        mm(o[:, 0:FF], lhsT=xqT[i], rhs=wgT[:], start=True, stop=True)
                        mm(o[:, 512:512 + FF], lhsT=xqT[i], rhs=wuT[:], start=True, stop=True).then_inc(W.full_of(step), 1)
                    elif k == "hT":
                        o = T.tile(step)
                        pe.wait_ge(*sigs["hq_ready"].count(g, (s, i // JH)))
                        for b in range(3):
                            n, at = min(D, FF - D * b), FF * (i % JH) + D * b
                            last = pe.transpose(o[0:n, D * b:D * b + D], hq[i // JH][:, at:at + n], ident)
                        last.then_inc(T.full_of(step), 1)
                    else:
                        o = T.tile(step)
                        pe.wait_ge(*sigs["hqT_part"].count(g, (s, i)))
                        for due in T.taken(pe, g, (s, "hT", i)):
                            pe.wait_ge(*due)
                        for b in range(3):
                            n = min(D, FF - D * b)
                            last = mm(o[:, 0:D], lhsT=hqT[i][0:n, D * b:D * b + D], rhs=wdT[0:n, b, :], start=b == 0, stop=b == 2)
                        last.then_inc(T.full_of(step), 1)
                elif s == "A":
                    if k in ("qk0", "qk1"):
                        turned(pe, g, s, i)
                        mm(T.tile(step)[:, 0:JH * S], lhsT=w("A_qkT" if k == "qk0" else "A_kqT"),
                                    rhs=half(xT, i).rearrange("p j t -> p (j t)"), start=True, stop=True) \
                        .then_inc(T.full_of(step), 1)
                    elif k == "dots":
                        j, c0 = i // US, CU * (i % US)
                        o, h = W.tile(step), i // (US * JH)
                        if i % (US * JH) == 0:
                            pe.wait_ge(qk_rows_loaded[h], 16 * 2 * ROWS * (g + 1))
                            pe.wait_ge(loadedb, 16)
                        for b in range(2):
                            mm(o[:, 512 * b:512 * b + 512], lhsT=causal, rhs=identb.unsqueeze(1).to_broadcast([128, 4, 128]),
                               start=True, stop=False, skip_group_check=True)
                            for n in range(4):
                                c = c0 + 4 * b + n
                                p, f = 32 * (c // CR), JH * S * (c % CR) + 128 * (j % JH)
                                last = mm(o[:, 512 * b + 128 * n:512 * b + 128 * n + 128], lhsT=KR[h][p:p + ROWS, f:f + 128],
                                          rhs=QR[h][p:p + ROWS, f:f + 128], start=False, stop=n == 3, skip_group_check=True)
                        last.then_inc(W.full_of(step), 1)
                    elif k == "apv":
                        j, q0 = i // US, CU // 4 * (i % US)
                        key = ("A", "apv", US * j)
                        if q0 == 0:
                            for due in P.emptied(pe, g, key):
                                pe.wait_ge(*due)
                            pe.wait_ge(*sigs["ones_spread"].count(g, (s, j)))
                            pe.wait_ge(*sigs["values_spread"].count(g, (s, j)))
                        for due in W.taken(pe, g, (s, "dots", i)):
                            pe.wait_ge(*due)
                        for b in range(2):
                            last = mm(P.tile(key)[:], lhsT=VZ[:, j, q0 + b, :], rhs=Sb[score_of[s, i]][:, 512 * b:512 * b + 512],
                                      start=q0 + b == 0, stop=q0 + b == QD - 1, skip_group_check=True)
                        if q0 + 2 == QD:
                            last.then_inc(P.full_of(key), 1)
                    else:
                        for due in P.taken(pe, g, (s, "apv", US * i)):
                            pe.wait_ge(*due)
                        pe.transpose(T.tile(step)[:, 0:D], RES[:, i, :], ident).then_inc(T.full_of(step), 1)
                elif s == "E":
                    if k == "rt":
                        o = T.tile(step)
                        turned(pe, g, s, i)
                        for j in range(JH):
                            mm(o[:, 12 * j:12 * j + 12], lhsT=xT[:, JH * i + j, :], rhs=w("E_r"), start=True, stop=False)
                            last = mm(o[:, 12 * j:12 * j + 12], lhsT=ones1, rhs=w("E_rb", 1), start=False, stop=True)
                        last.then_inc(T.full_of(step), 1)
                    elif k == "cT":
                        o = T.tile(step)
                        pe.wait_ge(*sigs["combine_ready"].count(g, (s, i)))
                        for j in range(JH):
                            last = pe.transpose(o[0:NE, 128 * j:128 * j + 128], combine[:, JH * i + j, :], ident)
                        last.then_inc(T.full_of(step), 1)
                    elif k == "h":
                        h, f = i // (2 * NE), i % (2 * NE)
                        pe.wait_ge(experts_loaded, 16 * (g + 1))
                        turned(pe, g, s, h)
                        mm(T.tile(step)[:, 0:JH * S], lhsT=ew1[:, 128 * f:128 * f + 128],
                                    rhs=half(xT, h).rearrange("p j t -> p (j t)"), start=True, stop=True) \
                        .then_inc(T.full_of(step), 1)
                    elif k == "y":
                        o, key, h, j = W.tile(step), ("E", "b2", i), i // JH, i % JH
                        for due in T.taken(pe, g, *[(s, "h", 2 * NE * (h + 1) - n) for n in (1, 2)], (s, "cT", h)):
                            pe.wait_ge(*due)
                        mm(P.tile(key)[:, 0:D], lhsT=combineT[0:NE, 128 * i:128 * i + 128], rhs=w("E_b2", NE),
                                    start=True, stop=True).then_inc(P.full_of(key), 1)
                        for e in range(NE):
                            for b in range(2):
                                f = 2 * e + b
                                last = mm(o[:, D * e:D * e + D], lhsT=HID[h][:, f, 128 * j:128 * j + 128],
                                          rhs=ew2[:, D * f:D * f + D], start=b == 0, stop=b == 1)
                        last.then_inc(W.full_of(step), 1)

            for ring in (W, T, P):
                for p in range(2):
                    pe.sem_inc(ring.free[p], 1)
            pe.wait_ge(loaded1, 16)
            for step in SETUP:
                fill(0, step)
            for due in T.taken(pe, 0, *SETUP[-2:]):
                pe.wait_ge(*due)
            pe.wait_ge(loaded2, 16)
            with pe.Fori(0, NG) as g:
                for step in steps:
                    fill(g, step)

        @block.scalar
        def _(act):
            A = nc.scalar.activation
            act.dma_start(wt2[:], t["weights2"]).then_inc(loaded2, 16)

            def take(g, step):
                s, k, i = step
                if s == "setup":
                    if k == "rel":
                        for due in T.filled(act, 0, step):
                            act.wait_ge(*due)
                        ins = nc.scalar.copy(relT[:, i, :], T.tile(step)[:, 0:D])
                        ins.then_inc(T.free_of(step), 1)
                    if k in ("gate", "up", "down"):
                        for due in T.filled(act, 0, step):
                            act.wait_ge(*due)
                        o = T.tile(step)
                        n = min(D, FF - D * i)
                        if k == "down":
                            ins = nc.scalar.copy(wdT[0:n, i, :], o[0:n, 0:D])
                        else:
                            ins = nc.scalar.copy((wgT if k == "gate" else wuT)[:, D * i:D * i + n], o[:, 0:n])
                        ins.then_inc(T.free_of(step), 1)
                    return
                if k == "xT":
                    for due in T.filled(act, g, step):
                        act.wait_ge(*due)
                    ins = nc.scalar.copy(xqT[i] if s == "F" else xT[:, i, :], T.tile(step)[:, 0:D])
                    ins.then_inc(T.free_of(step), 1)
                elif k in ("q", "k"):
                    for due in T.filled(act, g, step):
                        act.wait_ge(*due)
                    o = T.tile(step)[:, 0:JH * S]
                    if k == "q" and s != "X":
                        act.wait_ge(set_bias, 2)
                    dst = half(qT if k == "q" else kT, i).rearrange("p j t -> p (j t)")
                    if s == "X":
                        ins = A(dst, o, ACT.Copy, scale=float(qscale[s]) if k == "q" else 1.0)
                    else:
                        ins = A(dst, o, ACT.Identity, bias=bcol[s][0 if k == "q" else 1],
                                scale=float(qscale[s]) if k == "q" else 1.0)
                    ins.then_inc(T.free_of(step), 1)
                elif k == "v" and s != "R":
                    for due in T.filled(act, g, step):
                        act.wait_ge(*due)
                    if s == "A":
                        ins = nc.scalar.copy(half(VA, i), T.tile(step)[:, 0:JH * C].rearrange("p (j c) -> p j c", j=JH))
                    else:
                        ins = nc.scalar.copy(V[:, JH * i:JH * i + JH, :, 0:DH],
                                             T.tile(step)[:, 0:JH * D].rearrange("p (j h d) -> p j h d", j=JH, h=H))
                    ins.then_inc(T.free_of(step), 1)
                elif k == "c2p":
                    for due in W.filled(act, g, step):
                        act.wait_ge(*due)
                    ins = nc.scalar.copy(c2pb[:, :, 16 * i:16 * i + 16], W.tile(step)[:].rearrange("p (q b) -> p b q", q=16))
                    ins.then_inc(W.free_of(step), 1)
                elif k == "qk":
                    if s == "M":
                        for due in W.taken(act, g, step):
                            act.wait_ge(*due)
                    else:
                        act.wait_ge(*sigs["centred"].count(g, (s, i)))
                    x = Sb[score_of[s, i]][:]
                    A(x, x, ACT.Exp).then_inc(sigs["probs_ready"].next((s, i)), 1)
                elif k == "tr":
                    for b in range(2):
                        key = (s, "tr", 2 * i + b)
                        for due in T.filled(act, g, key):
                            act.wait_ge(*due)
                        ins = nc.scalar.copy(ET[weight_of[s, i]][:, 512 * b:512 * b + 512], T.tile(key)[:])
                        ins.then_inc(T.free_of(key), 1)
                elif k == "oT":
                    n = C if s == "A" else D
                    for due in T.filled(act, g, step):
                        act.wait_ge(*due)
                    ins = nc.scalar.copy(OT[0:n, i, :], T.tile(step)[0:n, 0:D])
                    ins.then_inc(T.free_of(step), 1)
                elif s == "R" and k == "cT":
                    for due in T.filled(act, g, step):
                        act.wait_ge(*due)
                    ins = nc.scalar.copy(ctxT[:, i, :], T.tile(step)[:, 0:D])
                    ins.then_inc(T.free_of(step), 1)
                elif s == "F" and k == "gu":
                    for due in W.filled(act, g, step):
                        act.wait_ge(*due)
                    A(eg[i // JH][:, FF * (i % JH):FF * (i % JH) + FF], W.tile(step)[:, 0:FF], ACT.Exp, scale=-1.0) \
                        .then_inc(sigs["eg_ready"].next((s, i)), 1)
                elif s == "F" and k == "hT":
                    for due in T.filled(act, g, step):
                        act.wait_ge(*due)
                    o = T.tile(step)
                    nc.scalar.copy(hqT[i][:, 0:2 * D], o[:, 0:2 * D]).then_inc(sigs["hqT_part"].next((s, i)), 1)
                    n = FF - 2 * D
                    ins = nc.scalar.copy(hqT[i][0:n, 2 * D:3 * D], o[0:n, 2 * D:3 * D])
                    ins.then_inc(T.free_of(step), 1)
                elif k == "dots":
                    for due in W.filled(act, g, step):
                        act.wait_ge(*due)
                    ins = A(Sb[score_of[s, i]][:], W.tile(step)[:], ACT.Exp)
                    ins.then_inc(W.free_of(step), 1)
                elif s == "E" and k == "rt":
                    act.wait_ge(*sigs["logits_ready"].count(g, (s, i)))
                    A(lexp, ldiff, ACT.Exp).then_inc(sigs["lexp_ready"].next((s, i)), 1)
                elif s == "E" and k == "cT":
                    for due in T.filled(act, g, step):
                        act.wait_ge(*due)
                    n = JH * S
                    ins = nc.scalar.copy(combineT[0:NE, n * i:n * i + n], T.tile(step)[0:NE, 0:n])
                    ins.then_inc(T.free_of(step), 1)
                elif k == "h":
                    for due in T.filled(act, g, step):
                        act.wait_ge(*due)
                    h, f = i // (2 * NE), i % (2 * NE)
                    ins = A(HID[h][:, f, :], T.tile(step)[:, 0:JH * S], ACT.Relu, bias=w("E_b1")[:, f:f + 1])
                    ins.then_inc(T.free_of(step), 1)

            for step in SETUP:
                take(None, step)
            act.wait_ge(loaded2, 16)
            act.wait_ge(loaded1, 16)
            act.wait_ge(set_pool, 3)
            with act.Fori(0, NG) as g:
                for step in steps:
                    take(g, step)

        @block.gpsimd
        def _(pool):
            nc.gpsimd.memset(halves[:], -0.5).then_inc(set_pool, 1)
            nc.gpsimd.memset(V[:], 1.0).then_inc(set_pool, 1)
            nc.gpsimd.memset(O[:], 0.0).then_inc(set_pool, 1)
            pool.wait_ge(loaded1, 16)
            pool.wait_ge(set_pool, 3)

            def root(g, step):
                pool.wait_ge(*sigs["var_ready"].count(g, step))
                j = step[2]
                nc.gpsimd.tensor_tensor(st[:, j, 9:10], st[:, j, 8:9], halves[:], ALU.pow).then_inc(sigs["rstd_ready"].next(step), 1)

            chain = [0]

            def link(ins, g):
                chain[0] += 1
                ins.then_inc(pool_chain, 1)
                pool.wait_ge(pool_chain, g * 4 * NH + chain[0])

            def help_(g, step):
                s, k, i = step
                if s == "L" and k == "q" and i == q_halves[0]:
                    for due in T.taken(pool, g, step):
                        pool.wait_ge(*due)
                    for j in range(JH * i, JH * i + JH):
                        ins = spread_queries(nc.gpsimd, j)
                    ins.then_inc(sigs["qexp_ready"].next((s, i)), 1)
                if k == "qk" and s in "LX":
                    pool.wait_ge(*sigs["summed"].count(g, (s, i)))
                    n = score_of[s, i]
                    v = Sb[n][:].rearrange("p (h k) -> p h k", h=HU)
                    nc.gpsimd.tensor_tensor(
                        v, v, small[:, 8 * n:8 * n + 8].unsqueeze(2).to_broadcast([128, HU, S]), ALU.subtract).then_inc(sigs["centred"].next((s, i)), 1)
                if s == "A" and k == "qk1":
                    pool.wait_ge(*sigs["kk_ready"].count(g, (s, i)))
                    KK, KRR = asplit[i][5], asplit[i][6]
                    kk, kr, kp = KK[0:C], KRR[0:C], kpart[i]
                    onec = w("ones", C)[:, 0:1].to_broadcast([C, JH * S])
                    link(nc.gpsimd.tensor_tensor(kp[0:C, 0], kk, onec, ALU.mult), g)
                    link(nc.gpsimd.tensor_tensor(kr, kk, kp[0:C, 0], ALU.subtract), g)
                    link(nc.gpsimd.tensor_tensor(kp[0:C, 1], kr, onec, ALU.mult), g)
                    link(nc.gpsimd.tensor_tensor(kr, kr, kp[0:C, 1], ALU.subtract), g)
                    nc.gpsimd.tensor_tensor(kp[0:C, 2], kr, onec, ALU.mult).then_inc(sigs["ksplit_ready"].next((s, i)), 1)
                if s == "A" and k == "v":
                    for due in T.taken(pool, g, step):
                        pool.wait_ge(*due)
                    qm = w("qmask").rearrange("p (q r) -> p q r", q=QD).unsqueeze(3).to_broadcast([128, QD, QD, 4])
                    for j in range(JH * i, JH * i + JH):
                        for give, at, x in (("ones_spread", C, w("ones")[:, 0:C]), ("values_spread", 0, VA[:, j, :])):
                            src = x.rearrange("p (r s) -> p r s", s=4).unsqueeze(1).to_broadcast([128, QD, QD, 4])
                            nc.gpsimd.tensor_tensor(
                                VZ[:, j, :, at:at + C].rearrange("p q (r s) -> p q r s", s=4), src, qm, ALU.mult).then_inc(sigs[give].next((s, j)), 1)
                if step in sigs["var_ready"].at:
                    root(g, step)

            with pool.Fori(0, NG) as g:
                for step in steps:
                    help_(g, step)

        @block.vector
        def _(dve):
            v = nc.vector
            chain = [0]

            def link(ins):
                chain[0] += 1
                ins.then_inc(dve_chain, 1)
                dve.wait_ge(dve_chain, chain[0])

            def quantise(dst, src, n, give=None):
                nb = n // QB
                a, r1, t1, q1 = (x[:, 0:n] for x in (f1, f2, f3, f4))
                amax, sc, rs = (fsm[:, JH * FF // QB * i:JH * FF // QB * i + nb] for i in range(3))

                def blocks(x):
                    return x.rearrange("p (b q) -> p b q", q=QB)

                def spread(x):
                    return x.unsqueeze(2).to_broadcast([128, nb, QB])
                link(v.tensor_reduce(amax, blocks(src), AX.X, ALU.max, apply_absolute_value=True))
                link(v.tensor_scalar(sc, amax, 1.0 / 6.0, 1e-12, ALU.mult, ALU.max))
                link(v.reciprocal(rs, sc))
                link(v.tensor_tensor(blocks(q1), blocks(src), spread(rs), ALU.mult))
                link(v.tensor_scalar(a.bitcast(I32), q1.bitcast(I32), 0x7FFFFFFF, None, ALU.bitwise_and))
                link(v.tensor_scalar(t1, a, 5.0, 2.0, ALU.is_gt, ALU.mult))
                link(v.tensor_scalar(r1, a, 1.75, None, ALU.is_gt))
                link(v.scalar_tensor_tensor(t1, a, 3.5, t1, ALU.is_gt, ALU.add))
                link(v.scalar_tensor_tensor(r1, a, 1.25, r1, ALU.is_gt, ALU.add))
                link(v.scalar_tensor_tensor(t1, a, 2.5, t1, ALU.is_gt, ALU.add))
                link(v.scalar_tensor_tensor(r1, a, 0.75, r1, ALU.is_gt, ALU.add))
                link(v.scalar_tensor_tensor(r1, a, 0.25, r1, ALU.is_gt, ALU.add))
                link(v.scalar_tensor_tensor(r1, r1, 0.5, t1, ALU.mult, ALU.add))
                link(v.tensor_tensor(blocks(a), blocks(r1), spread(sc), ALU.mult))
                give(v.scalar_tensor_tensor(dst.bitcast(I32), src.bitcast(I32), -2 ** 31, a.bitcast(I32),
                                            ALU.bitwise_and, ALU.bitwise_or))

            def normalise(g, step, res, out, gain=None, give=None):
                j = step[2]
                link(v.bn_stats(st[:, j, 0:6], res))
                link(v.bn_aggr(st[:, j, 6:8], st[:, j, 0:6]))
                ins = v.tensor_scalar(st[:, j, 8:9], st[:, j, 7:8], EPS, None, ALU.add)
                ins.then_inc(sigs["var_ready"].next(step), 1)
                dve.wait_ge(*sigs["rstd_ready"].count(g, step))
                dst = out if gain is None else res
                ins = v.tensor_scalar(dst, res, st[:, j, 6:7], st[:, j, 9:10], ALU.subtract, ALU.mult)
                if gain:
                    link(ins)
                    link(v.tensor_tensor(res, res, w(gain + "g"), ALU.mult))
                    ins = v.tensor_tensor(out, res, w(gain + "b"), ALU.add)
                if give:
                    ins.then_inc(sigs["x_ready"].next(give), 1)
                else:
                    link(ins)

            def setup():
                dve.wait_ge(loaded1, 16)
                dve.wait_ge(loaded2, 16)
                dve.wait_ge(set_pool, 3)
                v.tensor_scalar(scal[:, 0:1], w("bq"), float(qscale["L"]), None, ALU.mult).then_inc(set_bias, 1)
                v.tensor_scalar(scal[:, 2:3], w("M_bq"), float(qscale["M"]), None, ALU.mult).then_inc(set_bias, 1)
                for i, dst in enumerate((PK, PQ)):
                    step = ("setup", "pos", i)
                    for due in T.filled(dve, 0, step):
                        dve.wait_ge(*due)
                    ins = v.tensor_scalar(dst[:, 63:191] if i == 0 else dst[:, 64:192], T.tile(step)[:, 0:D],
                                          w("bpq" if i else "bpk"), float(qscale["L"]) if i else 1.0, ALU.add, ALU.mult)
                    ins.then_inc(T.free_of(step), 1)
                    for due in T.taken(dve, 0, step):
                        dve.wait_ge(*due)
                    lo = 63 if i == 0 else 64
                    link(v.tensor_copy(dst[:, 0:lo], dst[:, lo:lo + 1].to_broadcast([128, lo])))
                    hi = lo + D
                    v.tensor_copy(dst[:, hi:2 * S], dst[:, hi - 1:hi].to_broadcast([128, 2 * S - hi])).then_inc(set_pext, 1)
                dve.wait_ge(loaded3, 16)
                for name, buf in (("wgate", Sb[0][:, 0:384]), ("wup", Sb[0][:, 512:896])):
                    for i in range(3):
                        quantise(buf[:, D * i:D * i + D], raw[:, c3[name][0] + D * i:c3[name][0] + D * i + D], D, lambda ins: ins.then_inc(set_q, 1))
                quantise(Sb[1][:, 0:FF], raw[:, c3["wdown"][0]:n3], FF, lambda ins: ins.then_inc(set_q, 1))

            def work(g, step):
                s, k, i = step
                if s == "L" and k == "q" and i == q_halves[1]:
                    for due in T.taken(dve, g, step):
                        dve.wait_ge(*due)
                    for j in range(JH * i, JH * i + JH):
                        ins = spread_queries(v, j)
                    ins.then_inc(sigs["qexp_late_ready"].next((s, i)), 1)
                elif s in "LXM" and k == "k":
                    for due in T.taken(dve, g, step):
                        dve.wait_ge(*due)
                    for j in range(JH * i, JH * i + JH):
                        v.tensor_tensor(
                            kexp4[:, j], kT[:, j, :].unsqueeze(1).to_broadcast([128, H, S]),
                            w("hmask").unsqueeze(2).to_broadcast([128, H, S]), ALU.mult).then_inc(sigs["kexp_ready"].next((s, j)), 1)
                elif k == "p2c":
                    for due in W.filled(dve, g, step):
                        dve.wait_ge(*due)
                    ins = v.tensor_copy(p2cb[:, :, 16 * i:16 * i + 16], W.tile(step)[:].rearrange("p (q b) -> p b q", q=16))
                    ins.then_inc(W.free_of(step), 1)
                    for due in W.taken(dve, g, step):
                        dve.wait_ge(*due)
                elif k == "qk" and s in "LXM":
                    j, h0 = i // 2, HU * (i % 2)
                    cmask = cmasks[:, i // UH, :]
                    if s == "X" and i % 2 == 0:
                        if i % UH == 0:
                            dve.wait_ge(mask_loaded, 16 * (g + 1))
                        link(v.scalar_tensor_tensor(cmask, maskt[:, j, :], 0.0, w("window"), ALU.is_equal, ALU.mult))
                    for due in W.filled(dve, g, step):
                        dve.wait_ge(*due)
                    n = score_of[s, i]
                    sc = Sb[n][:].rearrange("p (h k) -> p h k", h=HU)
                    ps = W.tile(step)[:].rearrange("p (h k) -> p h k", h=HU)
                    mx = small[:, 8 * n:8 * n + 8]
                    if s == "M":
                        link(v.tensor_reduce(mx, ps, AX.X, ALU.max))
                        ins = v.tensor_tensor(sc, ps, mx.unsqueeze(2).to_broadcast([128, HU, S]), ALU.subtract)
                        ins.then_inc(W.free_of(step), 1)
                    else:
                        add = p2cb[:, H * j + h0:H * j + h0 + HU, :] if s == "L" else \
                            cmask.unsqueeze(1).to_broadcast([128, HU, S])
                        ins = v.tensor_tensor(sc, ps, add, ALU.add)
                        ins.then_inc(W.free_of(step), 1)
                        for due in W.taken(dve, g, step):
                            dve.wait_ge(*due)
                        v.tensor_reduce(mx, sc, AX.X, ALU.max).then_inc(sigs["summed"].next((s, i)), 1)
                elif k == "pv" and i % 2:
                    j, key = i // 2, (s, "pv", i - 1)
                    for due in P.filled(dve, g, key):
                        dve.wait_ge(*due)
                    o = P.tile(key)[:, 0:9 * H].rearrange("p (h d) -> p h d", h=H)
                    r = small[:, 16 + H * j:16 + H * j + H].unsqueeze(2)
                    link(v.reciprocal(r, o[:, :, DH:DH + 1]))
                    ins = v.tensor_tensor(O[:, j, :].rearrange("p (h d) -> p h d", h=H), o[:, :, 0:DH],
                                          r.to_broadcast([128, H, DH]), ALU.mult)
                    ins.then_inc(P.free_of(key), 1)
                elif k == "apv" and i % US == US - 1:
                    j = i // US
                    key = (s, "apv", US * j)
                    for due in P.filled(dve, g, key):
                        dve.wait_ge(*due)
                    o = P.tile(key)[:].rearrange("p (n i) -> p n i", n=4)
                    res = RES[:, j, :]
                    link(v.tensor_scalar(res, o[:, 0, :], w("smask")[:, 0:1], None, ALU.mult))
                    for n in range(1, 4):
                        ins = v.scalar_tensor_tensor(res, o[:, n, :], w("smask")[:, n:n + 1], res, ALU.mult, ALU.add)
                        if n < 3:
                            link(ins)
                    ins.then_inc(P.free_of(key), 1)
                elif k == "nT":
                    for due in T.filled(dve, g, step):
                        dve.wait_ge(*due)
                    r = small[:, 80 + C * i:80 + C + C * i]
                    link(v.reciprocal(r, T.tile(step)[:, C:2 * C]))
                    ins = v.tensor_tensor(O[:, i, 0:C], T.tile(step)[:, 0:C], r, ALU.mult)
                    ins.then_inc(T.free_of(step), 1)
                elif k == "oP" or (s, k) in (("R", "o"), ("F", "d")):
                    for due in T.filled(dve, g, step):
                        dve.wait_ge(*due)
                    if xin[s] == 0:
                        dve.wait_ge(x_loaded, 16 * (g + 1))
                    ins = v.tensor_tensor(RES[:, i, :], T.tile(step)[:, 0:D], xs[xin[s]][:, i, :], ALU.add)
                    ins.then_inc(T.free_of(step), 1)
                    for due in T.taken(dve, g, step):
                        dve.wait_ge(*due)
                    if (s, i) == first_out:
                        dve.wait_ge(stored, 16 * g + 16)
                    normalise(g, step, RES[:, i, :], xs[xin[s] + 1][:, i, :], "ln1" if s == "M" else None, (s, i))
                elif s == "R" and k == "s":
                    for due in T.filled(dve, g, step):
                        dve.wait_ge(*due)
                    ins = v.tensor_tensor(O[:, i, :], T.tile(step)[:, 0:D], w("decay"), ALU.mult)
                    ins.then_inc(T.free_of(step), 1)
                elif s == "R" and k == "v":
                    for due in T.filled(dve, g, step):
                        dve.wait_ge(*due)
                    r = small[:, 336 + i:337 + i]
                    link(v.tensor_scalar(r, T.tile(step)[:, 0:1], -1.0, 1.0, ALU.mult, ALU.max))
                    ins = v.tensor_tensor(r, T.tile(step)[:, 0:1], r, ALU.max)
                    ins.then_inc(T.free_of(step), 1)
                    for due in T.taken(dve, g, step):
                        dve.wait_ge(*due)
                    link(v.reciprocal(r, r))
                    v.tensor_scalar(OT[:, i, :], ctxt[:, i, :], r, None, ALU.mult).then_inc(sigs["cv_ready"].next((s, i)), 1)
                elif s == "F" and k == "xT" and i % JH == 0:
                    if xin[s]:
                        dve.wait_ge(*sigs["x_ready"].count(g, *[(stages[xin[s] - 1], j) for j in range(i, i + JH)]))
                    else:
                        dve.wait_ge(x_loaded, 16 * (g + 1))
                    quantise(xq[i // JH], xs[xin[s]][:, i:i + JH, :].rearrange("p j d -> p (j d)"), JH * D,
                             lambda ins: ins.then_inc(sigs["xq_ready"].next((s, i // JH)), 1))
                elif s == "F" and k == "gu":
                    o, h = W.tile(step), i // JH
                    e = eg[h][:, FF * (i % JH):FF * (i % JH) + FF]
                    dve.wait_ge(*sigs["eg_ready"].count(g, (s, i)))
                    for due in W.filled(dve, g, step):
                        dve.wait_ge(*due)
                    if i % JH == 0 and last_of[0] != (s, h):
                        dve.wait_ge(*sigs["hq_ready"].count(g, last_of[0]))
                    f = f1[:, 0:FF]
                    link(v.tensor_scalar(f, e, 1.0, None, ALU.add))
                    link(v.reciprocal(f, f))
                    link(v.tensor_tensor(f, f, o[:, 0:FF], ALU.mult))
                    v.tensor_tensor(e, f, o[:, 512:512 + FF], ALU.mult).then_inc(W.free_of(step), 1)
                    for due in W.taken(dve, g, step):
                        dve.wait_ge(*due)
                    if i % JH == JH - 1:
                        quantise(hq[h], eg[h], JH * FF, lambda ins: ins.then_inc(sigs["hq_ready"].next((s, h)), 1))
                elif s == "A" and k == "qk0":
                    for due in T.filled(dve, g, step):
                        dve.wait_ge(*due)
                    o = T.tile(step)[:, 0:JH * S]
                    QM, Q8, CMX, CMN, AR, KK = asplit[i][0:6]
                    link(v.tensor_scalar(QM[0:C], o[0:C], 0.125, None, ALU.mult))
                    ins = v.tensor_copy(KK[C:2 * C], o[C:2 * C])
                    ins.then_inc(T.free_of(step), 1)
                    for due in T.taken(dve, g, step):
                        dve.wait_ge(*due)
                elif s == "A" and k == "qk1":
                    for due in T.filled(dve, g, step):
                        dve.wait_ge(*due)
                    o = T.tile(step)[:, 0:JH * S]
                    QM, Q8, CMX, CMN, AR, KK = asplit[i][0:6]
                    v.tensor_copy(KK[0:C], o[0:C]).then_inc(sigs["kk_ready"].next((s, i)), 1)
                    ins = v.tensor_scalar(Q8[C:2 * C], o[C:2 * C], 0.125, None, ALU.mult)
                    ins.then_inc(T.free_of(step), 1)
                    for due in T.taken(dve, g, step):
                        dve.wait_ge(*due)
                    for j in range(JH):
                        f = slice(128 * j, 128 * j + 128)
                        kj = KK[C:2 * C, f]
                        link(v.tensor_tensor_scan(CMX[C:2 * C, f], kj, kj, -3.0e38, ALU.max, ALU.max))
                        link(v.tensor_tensor_scan(CMN[C:2 * C, f], kj, kj, 3.0e38, ALU.min, ALU.min))
                    hi = slice(C, 2 * C)
                    link(v.scalar_tensor_tensor(CMX[hi], Q8[hi], -1.0, CMX[hi], ALU.mult, ALU.mult))
                    link(v.scalar_tensor_tensor(CMN[hi], Q8[hi], -1.0, CMN[hi], ALU.mult, ALU.mult))
                    link(v.tensor_tensor(QM[hi], CMX[hi], CMN[hi], ALU.min))
                    link(v.tensor_copy(qpart[i][:, 0], QM))
                    link(v.tensor_tensor(AR, QM, qpart[i][:, 0], ALU.subtract))
                    link(v.tensor_copy(qpart[i][:, 1], AR))
                    link(v.tensor_tensor(AR, AR, qpart[i][:, 1], ALU.subtract))
                    v.tensor_copy(qpart[i][:, 2], AR).then_inc(sigs["qsplit_ready"].next((s, i)), 1)
                elif s == "E" and k == "rt":
                    for due in T.filled(dve, g, step):
                        dve.wait_ge(*due)
                    ins = v.tensor_copy(logits, T.tile(step)[:, 0:12 * JH])
                    ins.then_inc(T.free_of(step), 1)
                    for due in T.taken(dve, g, step):
                        dve.wait_ge(*due)
                    L = logits.rearrange("p (j n) -> p j n", j=JH)
                    Dl = ldiff.rearrange("p (j n) -> p j n", j=JH)
                    le = L[:, :, 4:12].rearrange("p j (g e) -> p j g e", e=2)
                    de = Dl[:, :, 4:12].rearrange("p j (g e) -> p j g e", e=2)
                    em4 = em.rearrange("p (j n) -> p j n", j=JH)
                    link(v.tensor_reduce(gm, L[:, :, 0:4], AX.X, ALU.max))
                    link(v.tensor_tensor(Dl[:, :, 0:4], L[:, :, 0:4], gm.unsqueeze(2).to_broadcast([128, JH, 4]), ALU.subtract))
                    link(v.tensor_tensor(em4, le[:, :, :, 0], le[:, :, :, 1], ALU.max))
                    link(v.tensor_tensor(de[:, :, :, 0], le[:, :, :, 0], em4, ALU.subtract))
                    v.tensor_tensor(de[:, :, :, 1], le[:, :, :, 1], em4, ALU.subtract).then_inc(sigs["logits_ready"].next((s, i)), 1)
                    oh4 = oh.rearrange("p (j n) -> p j n", j=JH)
                    EO = eo.rearrange("p (j g e) -> p j g e", j=JH, e=2)
                    link(v.tensor_tensor(oh4, L[:, :, 0:4], gm.unsqueeze(2).to_broadcast([128, JH, 4]), ALU.is_equal))
                    link(v.tensor_tensor(oh4, oh4, w("E_rank").unsqueeze(1).to_broadcast([128, JH, 4]), ALU.mult))
                    link(v.tensor_reduce(gm2, oh4, AX.X, ALU.max))
                    link(v.tensor_tensor(oh4, oh4, gm2.unsqueeze(2).to_broadcast([128, JH, 4]), ALU.is_equal))
                    link(v.tensor_tensor(EO[:, :, :, 0], le[:, :, :, 0], le[:, :, :, 1], ALU.is_ge))
                    link(v.tensor_scalar(EO[:, :, :, 1], EO[:, :, :, 0], -1.0, 1.0, ALU.mult, ALU.add))
                    dve.wait_ge(*sigs["lexp_ready"].count(g, (s, i)))
                    X = lexp.rearrange("p (j n) -> p j n", j=JH)
                    xe = X[:, :, 4:12].rearrange("p j (g e) -> p j g e", e=2)
                    link(v.tensor_reduce(gs, X[:, :, 0:4], AX.X, ALU.add))
                    link(v.tensor_tensor(em4, xe[:, :, :, 0], xe[:, :, :, 1], ALU.add))
                    link(v.reciprocal(gs, gs))
                    link(v.reciprocal(em, em))
                    link(v.tensor_tensor(em4, em4, gs.unsqueeze(2).to_broadcast([128, JH, 4]), ALU.mult))
                    link(v.tensor_tensor(em4, em4, oh4, ALU.mult))
                    cm = combine[:, JH * i:JH * i + JH, :].rearrange("p j (g e) -> p j g e", e=2)
                    link(v.tensor_tensor(cm[:, :, :, 0], EO[:, :, :, 0], em4, ALU.mult))
                    ins = v.tensor_tensor(cm[:, :, :, 1], EO[:, :, :, 1], em4, ALU.mult)
                    ins.then_inc(sigs["combine_ready"].next((s, i)), 1)
                    dve.wait_ge(*sigs["combine_ready"].count(g, (s, i)))
                elif s == "E" and k == "y":
                    res, key = RES[:, i, :], ("E", "b2", i)
                    for due in P.filled(dve, g, key):
                        dve.wait_ge(*due)
                    ins = v.tensor_tensor(res, P.tile(key)[:, 0:D], xs[xin[s]][:, i, :], ALU.add)
                    ins.then_inc(P.free_of(key), 1)
                    for due in P.taken(dve, g, key):
                        dve.wait_ge(*due)
                    for due in W.filled(dve, g, step):
                        dve.wait_ge(*due)
                    for e in range(NE):
                        ins = v.scalar_tensor_tensor(res, W.tile(step)[:, D * e:D * e + D], combine[:, i, e:e + 1], res,
                                                     ALU.mult, ALU.add)
                        if e < NE - 1:
                            link(ins)
                    ins.then_inc(W.free_of(step), 1)
                    for due in W.taken(dve, g, step):
                        dve.wait_ge(*due)
                    normalise(g, step, res, O[:, i, :], "ln2")
                elif k == "end":
                    link(v.tensor_tensor(RES[:, i, :], O[:, i, :], xs[xin["M"]][:, i, :], ALU.add))
                    if (s, i) == first_out:
                        dve.wait_ge(stored, 16 * g + 16)
                    normalise(g, step, RES[:, i, :], xs[NX][:, i, :], None, (s, i))

            setup()
            with dve.Fori(0, NG) as g:
                dve.sem_clear(dve_chain)
                chain[0] = 0
                for step in steps:
                    work(g, step)

        for name, x in sigs.items():
            assert x.given == len(x.keys), (name, x.given)


def shape_constants():
    at = np.arange(S)
    out = {"ident": np.eye(D), "anti": np.eye(D)[::-1], "ones": np.ones((128, D)),
           "hmask": (at[:, None] // DH == np.arange(H)[None, :]), "E_rank": np.tile(np.arange(4, 0, -1), (128, 1)),
           "window": np.where(abs(at[:, None] - at[None, :]) <= 64, MASKED / np.sqrt(float(D)), 0.0)}
    out["qmask"] = np.tile(np.eye(QD).reshape(1, -1), (128, 1))
    out["smask"] = (np.arange(128)[:, None] % 4 == np.arange(4)[None, :])
    dm = np.where(at[:, None] >= at[None, :], 0.96875 ** (at[None, :] - at[:, None]).astype(np.float64), 0.0)
    dm = dm / np.sqrt(dm.sum(axis=1)) / np.sqrt(float(D))
    out["decay"] = dm.T
    return {n: a.astype(np.float32) for n, a in out.items()}


STAGES = "LRFAXME"


def kernel(**inputs):
    import ml_dtypes
    import concourse.bacc as bacc
    from concourse.bass_utils import run_bass_kernel_spmd

    a = {n: np.asarray(x) for n, x in inputs.items()}
    f32 = np.float32

    def pack(fields, parts):
        at, n = columns(fields)
        out = np.zeros((128, n), f32)
        for name, (c, width) in at.items():
            x = parts[name]
            x = x.reshape(-1, 1) if x.ndim == 1 and width == 1 else np.atleast_2d(x)
            assert x.shape[1] == width, name
            out[0:x.shape[0], c:c + width] = x
        return out

    def rows3(x):
        out = np.zeros((3 * 128, D), f32)
        out[0:x.shape[0]] = x
        return out.reshape(3, 128, D).transpose(1, 0, 2).reshape(128, 3 * D)

    def by_head(x):
        out = np.zeros((D, D), f32)
        for h in range(H):
            out[DH * h:DH * h + DH, DH * h:DH * h + DH] = x.T
        return out

    def wide(x):
        return np.broadcast_to(x, (128, D))
    p = {n: x for n, x in shape_constants().items()}
    for n in ("Wq", "Wk", "Wv", "Wpk", "Wpq", "Wo"):
        p[n + "T"] = a["L0_attn_" + n].T
    for n in ("bq", "bk", "bpk", "bpq", "bv", "bo"):
        p[n] = a["L0_attn_" + n]
    p["rel"] = a["L0_attn_rel_emb"]
    p["wgate"], p["wup"], p["wdown"] = rows3(a["L0_ffn_w_gate"]), rows3(a["L0_ffn_w_up"]), a["L0_ffn_w_down"]
    wq, wk, wv = (a["L1_attn_w_qkv"][C * n:C * n + C].T for n in range(3))
    p["A_qkT"], p["A_kqT"], p["A_vT"] = np.concatenate([wq, wk], 1), np.concatenate([wk, wq], 1), wv
    p["A_oT"] = a["L1_attn_w_out"].T
    p["X_q"], p["X_k"], p["X_v"] = (by_head(a["L1_xattn_" + n]) for n in ("Wq", "Wk", "Wv"))
    p["X_oT"], p["X_bo"] = a["L1_xattn_Wo"].T, a["L1_xattn_bo"]
    e = "L1_ffn_"
    p["M_qT"], p["M_kT"], p["M_vT"] = (a[e + "in_proj_w"][D * n:D * n + D].T for n in range(3))
    p["M_bq"], p["M_bk"], p["M_bv"] = (a[e + "in_proj_b"][D * n:D * n + D] for n in range(3))
    p["M_oT"], p["M_bo"] = a[e + "out_proj_w"].T, a[e + "out_proj_b"]
    for n in ("ln1_g", "ln1_b", "ln2_g", "ln2_b"):
        p[n.replace("_", "")] = wide(a[e + n])
    p["E_r"] = np.concatenate([a[e + "w_group"], a[e + "w_expert"].transpose(1, 0, 2).reshape(D, NE)], 1)
    p["E_rb"] = np.concatenate([a[e + "b_group"], a[e + "b_expert"].reshape(NE)])
    p["E_w1"] = a[e + "w1"].transpose(1, 0, 2).reshape(D, NE * EF)
    p["E_b1"] = a[e + "b1"].reshape(2 * NE, 128).T
    p["E_w2"] = a[e + "w2"].reshape(2 * NE, 128, D).transpose(1, 0, 2).reshape(128, 2 * NE * D)
    p["E_b2"] = a[e + "b2"]

    bf = ml_dtypes.bfloat16
    at = np.arange(S)
    consts = np.concatenate([np.eye(D), np.where(at[None, :] > at[:, None], CAUSAL, 0.0)], 1).astype(bf)
    arrays = {"weights1": pack(FIRST, p), "weights2": pack(SECOND, p), "consts_bf16": consts, "raw": pack(RAW, p),
              "experts": pack(EXPERTS, p),
              "ones_rows": np.ones((RG, CR * JH * S), bf),
              "x": np.ascontiguousarray(a["x"]), "ctx": np.ascontiguousarray(a["ctx_1024"]),
              "mask": np.ascontiguousarray(a["mask_Bx1xSxS2_ff0"].reshape(B, S, S))}
    nc = bacc.Bacc("TRN2", target_bir_lowering=False, num_devices=1)
    t = {n: nc.dram_tensor("in_" + n, x.shape, mybir.dt.from_np(x.dtype), kind="ExternalInput").ap() for n, x in arrays.items()}
    t["out"] = nc.dram_tensor("out_0", (B, S, D), F32, kind="ExternalOutput").ap()
    t["q_rows"] = nc.dram_tensor("q_rows", (NH, 3, 2 * C, JH * S), BF16).ap()
    t["k_rows"] = nc.dram_tensor("k_rows", (NH, 3, C, JH * S), BF16).ap()
    build(nc, t, STAGES)
    r = run_bass_kernel_spmd(nc, [{"in_" + n: x for n, x in arrays.items()}], core_ids=[0])
    return r.results[0]["out_0"]
```
